# Optimizing a Trainium2 kernel written in Bass

```python
import numpy as np
import jax
import jax.numpy as jnp

def _softmax(x, axis=-1):
    return jax.nn.softmax(x, axis=axis)

def _gelu(x):
    return jax.nn.gelu(x, approximate=True)

def _silu(x):
    return jax.nn.silu(x)

def _sigmoid(x):
    return jax.nn.sigmoid(x)

def _layernorm(x, axis=-1, eps=1e-05):
    m = jnp.mean(x, axis=axis, keepdims=True)
    v = jnp.var(x, axis=axis, keepdims=True)
    return (x - m) / jnp.sqrt(v + eps)

def _scatter_add(tgt, idx, src, axis=0):
    return tgt.at[idx].add(src)

def _segment_sum(src, seg, n):
    return jax.ops.segment_sum(src, seg, n)
kernel_name = 'mk_perceiver_d1_seqx_r4_394631'

def setup_inputs(seed: int=0):
    np.random.seed(seed)
    _w = jnp.asarray

    def _rec_inputs():
        import jax
        import jax.numpy as jnp
        _rk = jax.random.key(seed)
        x = -0.000125 + 0.9999 * jax.random.normal(jax.random.fold_in(_rk, 1), (128, 32, 256), jnp.float32)
        _lenS = 32 - jax.random.randint(jax.random.fold_in(_rk, 7), (128,), 0, max(1, 32 // 4) + 1, jnp.int32)
        _lenS2 = 257 - jax.random.randint(jax.random.fold_in(_rk, 8), (128,), 0, max(1, 257 // 4) + 1, jnp.int32)
        _ctx_768P = jax.random.normal(jax.random.fold_in(_rk, 11), (128, 16, 192), jnp.float32)
        _ctx_768c = jax.random.dirichlet(jax.random.fold_in(_rk, 511), 0.3 * jnp.ones((16,), jnp.float32), (128, 257))
        _ctx_768t = jnp.einsum('bsk,bkd->bsd', _ctx_768c, _ctx_768P)
        _ctx_768t = _ctx_768t * jax.lax.rsqrt(jnp.mean(jnp.square(_ctx_768t)) + 1e-12) * 0.953939
        ctx_768 = 0.00272024 + 0.999456 * (_ctx_768t + 0.3 * jax.random.normal(jax.random.fold_in(_rk, 611), (128, 257, 192), jnp.float32))
        return (x, ctx_768)
    x, ctx_768 = _rec_inputs()

    def _L0_xattn_setup():
        import jax, jax.numpy as jnp
        import numpy as np
        QUERY_DIM = 256
        CONTEXT_DIM = 192
        HEADS = 8
        DIM_HEAD = 64
        INNER = HEADS * DIM_HEAD
        key = jax.random.key(seed)
        ks = jax.random.split(key, 7)
        B, S, L = (8, 1024, 77)
        x = jax.random.normal(ks[0], (B, S, QUERY_DIM), dtype=jnp.float32)
        context = jax.random.normal(ks[1], (B, L, CONTEXT_DIM), dtype=jnp.float32)
        Wq = jax.random.normal(ks[2], (QUERY_DIM, INNER), dtype=jnp.float32) * QUERY_DIM ** (-0.5)
        Wk = jax.random.normal(ks[3], (CONTEXT_DIM, INNER), dtype=jnp.float32) * CONTEXT_DIM ** (-0.5)
        Wv = jax.random.normal(ks[4], (CONTEXT_DIM, INNER), dtype=jnp.float32) * CONTEXT_DIM ** (-0.5)
        Wo = jax.random.normal(ks[5], (INNER, QUERY_DIM), dtype=jnp.float32) * INNER ** (-0.5)
        bo = jax.random.normal(ks[6], (QUERY_DIM,), dtype=jnp.float32) * 0.01
        return {'x': x, 'context': context, 'Wq': Wq, 'Wk': Wk, 'Wv': Wv, 'Wo': Wo, 'bo': bo}
    _L0_xattn_all = _L0_xattn_setup()
    _L0_xattn_in = {k: v for k, v in _L0_xattn_all.items() if k in ('Wq', 'Wk', 'Wv', 'Wo', 'bo')}
    del _L0_xattn_all

    def _L0_attn_setup():
        import jax, jax.numpy as jnp
        import numpy as np
        D = 256
        HS = 64
        H = D // HS
        B, T = (4, 512)
        EPS = 1e-05

        def _reference_tuple_inner(x, ln_g, ln_b, Wx, Ww, bw, Wk, Wv, Wr, Wo):
            Bb, Tt, C = x.shape
            nh, hs = (C // HS, HS)
            mu = x.mean(-1, keepdims=True)
            var = x.var(-1, keepdims=True)
            xn = (x - mu) / jnp.sqrt(var + EPS) * ln_g + ln_b
            w = jax.nn.sigmoid(xn @ Wx @ Ww + bw).reshape(Bb, Tt, nh, hs)
            k = (xn @ Wk).reshape(Bb, Tt, nh, hs)
            v = (xn @ Wv).reshape(Bb, Tt, nh, hs)
            r = jax.nn.sigmoid(xn @ Wr).reshape(Bb, Tt, nh, hs)

            def step(state, inp):
                kt, vt, wt, rt = inp
                state = (1.0 - wt)[..., None] * state + kt[..., None] * vt[..., None, :]
                out = jnp.einsum('bhd,bhde->bhe', rt, state)
                return (state, out)
            init = jnp.zeros((Bb, nh, hs, hs), x.dtype)
            tm = lambda a: jnp.moveaxis(a, 1, 0)
            state, outs = jax.lax.scan(step, init, (tm(k), tm(v), tm(w), tm(r)))
            y = jnp.moveaxis(outs, 0, 1).reshape(Bb, Tt, C) @ Wo
            return (y, state)
        key = jax.random.key(seed)
        ks = jax.random.split(key, 8)
        s = 1.0 / np.sqrt(D)
        mk = lambda k: jax.random.normal(k, (D, D), jnp.float32) * s
        return {'x': jax.random.normal(ks[0], (B, T, D), jnp.float32), 'ln_g': jnp.ones((D,), jnp.float32), 'ln_b': jnp.zeros((D,), jnp.float32), 'Wx': mk(ks[1]), 'Ww': mk(ks[2]), 'bw': jnp.zeros((D,), jnp.float32), 'Wk': mk(ks[3]), 'Wv': mk(ks[4]), 'Wr': mk(ks[5]), 'Wo': mk(ks[6])}
    _L0_attn_all = _L0_attn_setup()
    _L0_attn_in = {k: v for k, v in _L0_attn_all.items() if k in ('ln_g', 'ln_b', 'Wx', 'Ww', 'bw', 'Wk', 'Wv', 'Wr', 'Wo')}
    del _L0_attn_all

    def _L0_ffn_setup():
        import jax, jax.numpy as jnp
        import numpy as np
        D_MODEL, D_FF, RANK = (256, 1024, 64)
        B, S = (4, 1024)
        key = jax.random.key(seed)
        ks = jax.random.split(key, 7)
        return {'x': jax.random.normal(ks[0], (B, S, D_MODEL), dtype=jnp.float32), 'U1': jax.random.normal(ks[1], (D_MODEL, RANK), dtype=jnp.float32) * 0.02, 'V1': jax.random.normal(ks[2], (RANK, D_FF), dtype=jnp.float32) * 0.02, 'b1': jnp.zeros((D_FF,), dtype=jnp.float32), 'U2': jax.random.normal(ks[3], (D_FF, RANK), dtype=jnp.float32) * 0.02, 'V2': jax.random.normal(ks[4], (RANK, D_MODEL), dtype=jnp.float32) * 0.02, 'b2': jnp.zeros((D_MODEL,), dtype=jnp.float32)}
    _L0_ffn_all = _L0_ffn_setup()
    _L0_ffn_in = {k: v for k, v in _L0_ffn_all.items() if k in ('U1', 'V1', 'b1', 'U2', 'V2', 'b2')}
    del _L0_ffn_all
    return {'x': x, 'ctx_768': ctx_768, 'L0_xattn_Wq': _L0_xattn_in['Wq'], 'L0_xattn_Wk': _L0_xattn_in['Wk'], 'L0_xattn_Wv': _L0_xattn_in['Wv'], 'L0_xattn_Wo': _L0_xattn_in['Wo'], 'L0_xattn_bo': _L0_xattn_in['bo'], 'L0_attn_ln_g': _L0_attn_in['ln_g'], 'L0_attn_ln_b': _L0_attn_in['ln_b'], 'L0_attn_Wx': _L0_attn_in['Wx'], 'L0_attn_Ww': _L0_attn_in['Ww'], 'L0_attn_bw': _L0_attn_in['bw'], 'L0_attn_Wk': _L0_attn_in['Wk'], 'L0_attn_Wv': _L0_attn_in['Wv'], 'L0_attn_Wr': _L0_attn_in['Wr'], 'L0_attn_Wo': _L0_attn_in['Wo'], 'L0_ffn_U1': _L0_ffn_in['U1'], 'L0_ffn_V1': _L0_ffn_in['V1'], 'L0_ffn_b1': _L0_ffn_in['b1'], 'L0_ffn_U2': _L0_ffn_in['U2'], 'L0_ffn_V2': _L0_ffn_in['V2'], 'L0_ffn_b2': _L0_ffn_in['b2']}

def reference(x, ctx_768, L0_xattn_Wq, L0_xattn_Wk, L0_xattn_Wv, L0_xattn_Wo, L0_xattn_bo, L0_attn_ln_g, L0_attn_ln_b, L0_attn_Wx, L0_attn_Ww, L0_attn_bw, L0_attn_Wk, L0_attn_Wv, L0_attn_Wr, L0_attn_Wo, L0_ffn_U1, L0_ffn_V1, L0_ffn_b1, L0_ffn_U2, L0_ffn_V2, L0_ffn_b2):
    import jax
    import jax.numpy as jnp

    def _L0_xattn_ref(x, context, Wq, Wk, Wv, Wo, bo):
        import jax, jax.numpy as jnp
        import numpy as np
        QUERY_DIM = 256
        CONTEXT_DIM = 192
        HEADS = 8
        DIM_HEAD = 64
        INNER = HEADS * DIM_HEAD
        B, S, _ = x.shape
        L = context.shape[1]
        scale = DIM_HEAD ** (-0.5)
        q = (x @ Wq).reshape(B, S, HEADS, DIM_HEAD).transpose(0, 2, 1, 3)
        k = (context @ Wk).reshape(B, L, HEADS, DIM_HEAD).transpose(0, 2, 1, 3)
        v = (context @ Wv).reshape(B, L, HEADS, DIM_HEAD).transpose(0, 2, 1, 3)
        attn = jnp.einsum('bhsd,bhld->bhsl', q, k) * scale
        attn = jax.nn.softmax(attn, axis=-1)
        out = jnp.einsum('bhsl,bhld->bhsd', attn, v)
        out = out.transpose(0, 2, 1, 3).reshape(B, S, INNER)
        return out @ Wo + bo

    def _L0_attn_ref(x, ln_g, ln_b, Wx, Ww, bw, Wk, Wv, Wr, Wo):
        import jax, jax.numpy as jnp
        import numpy as np
        D = 256
        HS = 64
        H = D // HS
        B, T = (4, 512)
        EPS = 1e-05

        def _reference_tuple_inner(x, ln_g, ln_b, Wx, Ww, bw, Wk, Wv, Wr, Wo):
            Bb, Tt, C = x.shape
            nh, hs = (C // HS, HS)
            mu = x.mean(-1, keepdims=True)
            var = x.var(-1, keepdims=True)
            xn = (x - mu) / jnp.sqrt(var + EPS) * ln_g + ln_b
            w = jax.nn.sigmoid(xn @ Wx @ Ww + bw).reshape(Bb, Tt, nh, hs)
            k = (xn @ Wk).reshape(Bb, Tt, nh, hs)
            v = (xn @ Wv).reshape(Bb, Tt, nh, hs)
            r = jax.nn.sigmoid(xn @ Wr).reshape(Bb, Tt, nh, hs)

            def step(state, inp):
                kt, vt, wt, rt = inp
                state = (1.0 - wt)[..., None] * state + kt[..., None] * vt[..., None, :]
                out = jnp.einsum('bhd,bhde->bhe', rt, state)
                return (state, out)
            init = jnp.zeros((Bb, nh, hs, hs), x.dtype)
            tm = lambda a: jnp.moveaxis(a, 1, 0)
            state, outs = jax.lax.scan(step, init, (tm(k), tm(v), tm(w), tm(r)))
            y = jnp.moveaxis(outs, 0, 1).reshape(Bb, Tt, C) @ Wo
            return (y, state)
        return _reference_tuple_inner(x, ln_g, ln_b, Wx, Ww, bw, Wk, Wv, Wr, Wo)[0]

    def _L0_ffn_ref(x, U1, V1, b1, U2, V2, b2):
        import jax, jax.numpy as jnp
        import numpy as np
        D_MODEL, D_FF, RANK = (256, 1024, 64)
        B, S = (4, 1024)
        P = jnp.einsum('bsd,dr->bsr', x, U1)
        H = jax.nn.gelu(jnp.einsum('bsr,rf->bsf', P, V1) + b1)
        Q = jnp.einsum('bsf,fr->bsr', H, U2)
        return jnp.einsum('bsr,rd->bsd', Q, V2) + b2
    x = x + _L0_xattn_ref(_layernorm(x, axis=-1), ctx_768, L0_xattn_Wq, L0_xattn_Wk, L0_xattn_Wv, L0_xattn_Wo, L0_xattn_bo)
    x = x + _L0_attn_ref(_layernorm(x, axis=-1), L0_attn_ln_g, L0_attn_ln_b, L0_attn_Wx, L0_attn_Ww, L0_attn_bw, L0_attn_Wk, L0_attn_Wv, L0_attn_Wr, L0_attn_Wo)
    x = x + _L0_ffn_ref(_layernorm(x, axis=-1), L0_ffn_U1, L0_ffn_V1, L0_ffn_b1, L0_ffn_U2, L0_ffn_V2, L0_ffn_b2)
    return x

_drawn_inputs = setup_inputs


def setup_inputs(seed=0):
    import zlib

    import numpy as np

    out = dict(_drawn_inputs(seed))
    spreads = {'L0_attn_ln_g': (1.0, 0.2),
     'L0_attn_ln_b': (0.0, 0.1),
     'L0_attn_bw': (0.0, 0.1),
     'L0_ffn_b1': (0.0, 0.8),
     'L0_ffn_b2': (0.0, 1.48)}
    factors = {'L0_xattn_bo': 3.958,
     'L0_ffn_U1': 8.0,
     'L0_ffn_V1': 8.0,
     'L0_ffn_U2': 8.0,
     'L0_ffn_V2': 8.0}
    for name, (base, spread) in spreads.items():
        noise = np.random.default_rng([zlib.crc32(name.encode()), seed]).standard_normal(out[name].shape)
        drawn = base * np.exp(spread * noise) if base else spread * noise
        out[name] = jnp.asarray(drawn.astype(out[name].dtype))
    for name, factor in factors.items():
        out[name] = (out[name] * factor).astype(out[name].dtype)
    return out
```

```python
from contextlib import ExitStack

import concourse.bass as bass
import concourse.mybir as mybir
import numpy as np

F32 = mybir.dt.float32
F32R = mybir.dt.float32r
U8 = mybir.dt.uint8
ACT = mybir.ActivationFunctionType
ALU = mybir.AluOpType
AX = mybir.AxisListType

B, S, D = 128, 32, 256
L, C = 257, 192
H, DH = 8, 64
INNER = H * DH
F, R = 1024, 64
G = 8
NG = B // G
T = G * S
P = 128
LP = L + 1
LT = 2
SCALE = DH ** -0.5
EPS = 1e-5
A_MIN = 2.0 ** -25
LEVELS = 4

START = ["WV0", "WV1", "XT", "WV2", "q0", "q1", "WV3", "Qk0", "Qk1", "q2", "Qk2", "Qk3", "q3",
         "Qk4", "Qk5", "Qk6", "Qk7", "Y1"]
FILL1 = [[], ["z"], ["r"], [], ["S0", "S1"], ["S4", "S5"], ["O2"], ["Pf", "H0"]]
FILL2 = [["XT2"], ["k"], ["v"], ["hats"], ["S2", "S3"], ["S6", "S7"], ["Y2", "XT3"],
         ["H1", "H2", "Qf0", "H3", "Qf1", "Y3"]]
A_STEPS = {"XT"} | {f"q{p}" for p in range(4)} | {f"Qk{h}" for h in range(H)}
NO_BANK = {"hats", "Qf1"}
BANK_ORDER = [("Qf" if n == "Qf0" else n) for n in
              START + [n for b in range(G) for n in FILL1[b] + FILL2[b]] if n not in NO_BANK]
BANKS = 4


class Group:

    def __init__(self, register, plus):
        self.register, self.plus = register, plus
        self.index = register + plus

    def at(self, per_group, k):
        return self.register * per_group + (self.plus * per_group + k)


class Phase:

    def __init__(self, which, m):
        self.which, self.m = which, m
        self.a = None if which == "last" else Group(m, 0 if which == "first" else 1)
        self.b = None if which == "first" else Group(m, 0)

    def has(self, name):
        return (self.a if name in A_STEPS else self.b) is not None


def order_of(which):
    return [n for n in BANK_ORDER if which == "middle" or (n in A_STEPS) == (which == "first")]


def bank_of(phase, name):
    return order_of(phase.which).index(name) % BANKS


def filled(phase, name, k=1):
    bank = bank_of(phase, name)
    here = order_of(phase.which).index(name) // BANKS + k
    first = len(order_of("first")[bank::BANKS])
    middle = len(order_of("middle")[bank::BANKS])
    if phase.which == "first":
        return here
    if phase.which == "middle":
        return phase.m * middle + (first + here)
    return first + (NG - 1) * middle + here


class Chain:

    def __init__(self, engine, sem, first, middle):
        self.engine, self.sem, self.sizes, self.k, self.base = engine, sem, (first, middle), 0, 0

    def begin(self, phase, start):
        self.k = 0
        first, middle = self.sizes
        self.base = start + (0 if phase.which == "first" else phase.m * middle + first)
        return self

    def link(self, instruction):
        instruction.then_inc(self.sem, 1)
        self.k += 1
        self.engine.wait_ge(self.sem, self.base + self.k)


DVE_LINKS = (27, 103)
POOL_LINKS = (0, 5)


def build(nc, a, out):
    with ExitStack() as ctx:
        def sb(name, shape, dt=F32):
            return ctx.enter_context(nc.sbuf_tensor(name, shape, dt))

        def ps(name, shape):
            return ctx.enter_context(nc.psum_tensor(name, shape, F32))

        def sem(name):
            return ctx.enter_context(nc.semaphore(name))

        wq_h, wq_l = sb("wq_h", [P, 2, INNER], F32R), sb("wq_l", [P, 2, INNER], F32R)
        wk_h, wk_l = sb("wk_h", [P, H, 256], F32R), sb("wk_l", [P, H, 256], F32R)
        wv_h, wv_l = sb("wv_h", [P, 2, H, P], F32R), sb("wv_l", [P, 2, H, P], F32R)
        wo_h, wo_l = sb("wo_h", [P, 4, D], F32R), sb("wo_l", [P, 4, D], F32R)
        w2 = sb("w2", [P, 3, 2, D])
        wz = sb("wz", [P, 2, D])
        wo2 = sb("wo2", [P, 2, D])
        u1, u2 = sb("u1", [P, 2, R]), sb("u2", [P, 8, R])
        v12 = sb("v12", [P, F])
        v1, v2 = v12[0:R], v12[R:2 * R, 0:D]
        bo, b2 = sb("bo", [P, D]), sb("b2", [P, D])
        vecs = sb("vecs", [P, 16])
        ident_r = sb("ident_r", [P, P], F32R)
        ident = ident_r[:].bitcast(F32)
        mask = sb("mask", [P, LEVELS, P], U8)

        raw_t = [sb(f"raw_t{i}", [P, 2, LP]) for i in range(2)]
        raw_n = [sb(f"raw_n{i}", [P, LT, C]) for i in range(2)]
        t0h = [sb(f"t0h{i}", [P, LP], F32R) for i in range(2)]
        t0l = [sb(f"t0l{i}", [P, LP], F32R) for i in range(2)]
        t1 = [sb(f"t1_{i}", [P, LP], F32R) for i in range(2)]
        t1s = sb("t1s", [P, LP], F32R)
        nat = [sb(f"nat{i}", [P, LT, 384], F32R) for i in range(2)]
        probs = sb("probs", [P, 2, LP])
        tailp = sb("tailp", [P, 2, P], F32R)
        pth, ptl = sb("pth", [P, LT, 256], F32R), sb("ptl", [P, LT, 256], F32R)
        ptt = sb("ptt", [3, 256], F32R)
        nmax, rsum, rinv = sb("nmax", [P, 2]), sb("rsum", [P, 2]), sb("rinv", [P, 2])

        cell, eps2 = sb("cell", [1, 1]), sb("eps2", [P, 2])

        tailc = sb("tailc", [3, G // 2, 256], F32R)
        xin, xb, x12 = (sb(n, [P, 2, D]) for n in ("xin", "xb", "x12"))
        xn = sb("xn", [P, 2, D])
        stats, mv = sb("stats", [P, 2, 6]), sb("mv", [P, 3, 2, 2])
        ve, rstd = sb("ve", [P, 3, 2]), sb("rstd", [P, 4, 2])
        at, kt, rt_, vt = (sb(n, [P, 2, T]) for n in ("at", "kt", "rt", "vt"))
        fw, bw_, pw = (sb(n, [P, 2 * T]) for n in ("fw", "bwd", "pw"))
        ob = at
        s2 = sb("s2", [P, 8, P])
        o2 = pw[:].rearrange("p (c t) -> p c t", c=2)
        pq = sb("pq", [P, T])
        pf, qf = pq[0:R], pq[R:2 * R]

        KB = 1024
        base = (nc.sbuf_usable_end - 80 * KB) // 32 * 32
        assert nc.sbuf_base <= base, (nc.sbuf_base, base)

        def at_(name, shape, dt, offset):
            return nc.alloc_sbuf_tensor_at(name, shape, dt, offset=base + offset)

        oh = at_("oh", [P, 4, T], F32R, 0)
        ol = at_("ol", [P, 4, T], F32R, 4096)
        qs = at_("qs", [P, 4, T], F32R, 8192)
        xth = at_("xth", [P, 2, T], F32R, 12288)
        xtl = at_("xtl", [P, 2, T], F32R, 14336)
        xt = at_("xt", [P, 2, T], F32, 12288)
        rhat = at_("rhat", [P, LEVELS, 2 * T], F32, 0)
        khat = at_("khat", [P, LEVELS, 2 * T], F32, 8192)
        hid = at_("hid", [P, 8, T], F32, 0)

        qk_h = at_("qk_h", [P, 2, G, 256], F32R, 16 * KB)
        qk_l = at_("qk_l", [P, 2, G, 256], F32R, 32 * KB)
        pc_h = at_("pc_h", [P, 2, H, T], F32R, 48 * KB)
        pc_l = at_("pc_l", [P, 2, H, T], F32R, 64 * KB)
        scores = ps("scores", [P, 2, 512])
        ptp = ps("ptp", [P, LT, 256])
        acc = ps("acc", [P, 2, 256])
        gb = [ps(f"gb{i}", [P, 2, 256]) for i in range(BANKS)]

        w_in, x_in, tailc_in, out_done, scratch_in = (sem(n) for n in
                                                      ("w_in", "x_in", "tailc_in", "out_done", "scratch_in"))
        ctxt_in = [sem(f"ctxt_in{i}") for i in range(2)]
        ctxn_in = [sem(f"ctxn_in{i}") for i in range(2)]
        bank_filled = [sem(f"bank_filled{i}") for i in range(BANKS)]
        bank_drained = [sem(f"bank_drained{i}") for i in range(BANKS)]
        names = ("weights_ready wz_psum wz_ready tail_split thi_ready tlo_ready nhi_ready nlo_ready "
                 "scores_ready nmax_ready exp_ready probs_ready tailt_ready ptt_ready pt_ready "
                 "pth_ready ptl_ready acc_ready pch_ready pcl_ready xthi_ready qhi_ready qkhi_ready "
                 "oh_ready xb_ready ob_ready var_ready rstd_ready xn_ready rhat_ready khat_ready r_ready "
                 "pw_ready dve_chain pool_chain pe_setup").split()
        s = {n: sem(n) for n in names}

        x_v = a["x"].rearrange("(g t p) d -> g p t d", g=NG, p=P)
        out_v = out.rearrange("(g t p) d -> g p t d", g=NG, p=P)
        ctxt_v, ctxn_v = a["ctx_t"], a["ctx_n"]
        scratch = nc.dram_tensor("tail_scratch", [3, B, 256], F32, kind="Internal").ap()

        wq_raw = at_("wq_raw", [P, 2, INNER], F32, 16 * KB)
        wo_raw = at_("wo_raw", [P, 4, D], F32, 20 * KB)
        wk_raw = at_("wk_raw", [P, H, 256], F32, 24 * KB)
        wv_raw = at_("wv_raw", [P, 2, H, P], F32, 32 * KB)
        wxt_raw = at_("wxt_raw", [P, 2, D], F32, 40 * KB)
        ww_raw = at_("ww_raw", [P, 2, D], F32, 42 * KB)
        tail_raw = at_("tail_raw", [P, C], F32, 44 * KB)
        tail3 = at_("tail3", [P, 3, 256], F32R, 48 * KB)
        bw_raw = at_("bw_raw", [P, 2], F32, 52 * KB)
        ident_raw = at_("ident_raw", [P, P], F32, 53 * KB)
        mask_raw = at_("mask_raw", [P, LEVELS, P], F32, 54 * KB)

        LOADS = [(wq_raw[:], a["wq"]), (wo_raw[:], a["wo"]), (wk_raw[:], a["wk"]), (wv_raw[:], a["wv"]),
                 (wxt_raw[:], a["wxt"]), (ww_raw[:], a["ww"]), (tail_raw[:], a["ctx_tail"]),
                 (w2[:, 0], a["wk2"]), (w2[:, 1], a["wv2"]), (w2[:, 2], a["wr2"]), (wo2[:], a["wo2"]),
                 (u1[:], a["u1"]), (v1, a["v1"]), (u2[:], a["u2"]), (v2, a["v2"]),
                 (bo[:], a["bo"]), (b2[:], a["b2"]), (vecs[:, 0:2], a["ln_g"]), (vecs[:, 2:4], a["ln_b"]),
                 (bw_raw[:], a["bw"]), (vecs[:, 6:14], a["b1"]), (ident_raw[:], a["ident"]),
                 (mask_raw[:], a["mask"])]
        W_ALL = 16 * len(LOADS)

        block = ctx.enter_context(nc.Block())

        def turns(engine, body):
            body(Phase("first", 0))
            with engine.Fori(0, NG - 1) as m:
                body(Phase("middle", m))
            body(Phase("last", NG - 1))

        @block.sync
        def _(sp):
            for dst, src in LOADS:
                sp.dma_start(dst, src).then_inc(w_in, 16)
            sp.wait_ge(s["tail_split"], 1)
            sp.dma_start(scratch.rearrange("r b c -> b r c"), tail3[:].bitcast(F32)).then_inc(scratch_in, 16)
            sp.wait_ge(scratch_in, 16)

            def body(ph):
                g = ph.a
                first = ph.which == "first"

                def load_t(b):
                    if not (first and b < 2):
                        sp.wait_ge(s["tlo_ready"], g.at(G, b - 1))
                    sp.dma_start(raw_t[b % 2][:], ctxt_v[g.index * G + b]).then_inc(ctxt_in[b % 2], 16)

                def load_n(b):
                    if not (first and b < 2):
                        sp.wait_ge(s["nlo_ready"], g.at(G, b - 1))
                    sp.dma_start(raw_n[b % 2][:], ctxn_v[g.index * G + b]).then_inc(ctxn_in[b % 2], 16)

                if not first:
                    sp.wait_ge(s["xb_ready"], g.at(1, 0))
                sp.dma_start(xin[:], x_v[g.index]).then_inc(x_in, 16)
                load_t(0)
                load_t(1)
                load_n(0)
                load_n(1)
                if not first:
                    sp.wait_ge(s["acc_ready"], g.at(G, 0))
                half = G // 2
                sp.dma_start(tailc[:].bitcast(F32), scratch[:, bass.ds(g.index * G, half)]).then_inc(tailc_in, 16)
                for b in range(2, G):
                    load_t(b)
                    if b == G - 1:
                        sp.wait_ge(s["acc_ready"], g.at(G, half))
                        sp.dma_start(tailc[:].bitcast(F32), scratch[:, bass.ds(g.index * G + half, half)])\
                            .then_inc(tailc_in, 16)
                    load_n(b)

            body(Phase("first", 0))
            with sp.Fori(0, NG - 1) as m:
                body(Phase("middle", m))

        @block.tensor
        def _(pe):
            mm = nc.tensor.matmul

            pe.wait_ge(w_in, W_ALL)
            for i in range(2):
                for j in range(2):
                    last = mm(gb[0][:, i], wxt_raw[:, j, i * P:(i + 1) * P], ww_raw[:, j], start=j == 0,
                              stop=j == 1)
            last.then_inc(s["wz_psum"], 1)
            pe.wait_ge(s["weights_ready"], 1)
            pe.wait_ge(s["tail_split"], 1)

            def body(ph):
                ga, gp = ph.a, ph.b
                taken = []

                def tile(name):
                    bank = bank_of(ph, name)
                    taken.append(name)
                    before = filled(ph, name, 0)
                    if not (isinstance(before, int) and before == 0):
                        pe.wait_ge(bank_drained[bank], before)
                    return gb[bank]

                def done(name, last):
                    last.then_inc(bank_filled[bank_of(ph, name)], 1)

                def drained(name):
                    order = order_of(ph.which)
                    ahead = order.index(taken[-1]) - order.index(name) if taken else 0
                    if ahead > 0 and ahead % BANKS == 0:
                        return
                    pe.wait_ge(bank_drained[bank_of(ph, name)], filled(ph, name))

                def turn(name):
                    g, ln = (ga, 0) if name == "XT" else (gp, int(name[2]) - 1)
                    out_ = tile(name)
                    pe.wait_ge(s["xn_ready"], xn_count(ph, ln))
                    for t in range(2):
                        for c in range(2):
                            last = nc.tensor.transpose(out_[:, c, t * P:(t + 1) * P],
                                                       xn[:, t, c * P:(c + 1) * P], ident)
                    done(name, last)

                def q(p):
                    out_ = tile(f"q{p}")
                    drained("XT")
                    k = 0
                    for c in range(2):
                        for w, x in ((wq_h, xth), (wq_l, xth), (wq_h, xtl)):
                            last = mm(out_[:, 0], w[:, c, p * P:(p + 1) * P], x[:, c], start=k == 0,
                                      stop=k == 5)
                            k += 1
                    done(f"q{p}", last)

                def qk(h):
                    out_ = tile(f"Qk{h}")
                    drained(f"q{h // 2}")
                    for c in range(2):
                        for k, w in enumerate((wk_h, wk_l)):
                            last = mm(out_[:, c], w[:, h, c * P:(c + 1) * P], qs[:, h % 4], start=k == 0,
                                      stop=k == 1)
                    done(f"Qk{h}", last)

                def score(b):
                    pe.wait_ge(s["tlo_ready"], ga.at(G, b + 1))
                    if b == 0:
                        drained("Qk7")
                    if not (ph.which == "first" and b == 0):
                        pe.wait_ge(s["ptt_ready"], ga.at(G, b))
                    for r in range(2):
                        o = scores[:, r, 0:LP]
                        r_ = slice(r * P, (r + 1) * P)
                        k = 0
                        for w, x in ((qk_h[:, 0, b, r_], t0h), (qk_l[:, 0, b, r_], t0h),
                                     (qk_h[:, 0, b, r_], t0l), (qk_h[:, 1, b, r_], t1),
                                     (qk_l[:, 1, b, r_], t1)):
                            last = mm(o, w, x[b % 2][:], start=k == 0, stop=k == 4)
                            k += 1
                        last.then_inc(s["scores_ready"], 1)

                def turn_probs(b):
                    pe.wait_ge(s["probs_ready"], ga.at(G, b + 1))
                    for r in range(2):
                        last = mm(scores[:, r, 384:512], tailp[:, r], ident_r[:], start=True, stop=True)
                    last.then_inc(s["tailt_ready"], 1)
                    if not (ph.which == "first" and b == 0):
                        pe.wait_ge(s["ptl_ready"], ga.at(G, b))
                    for r in range(2):
                        for t in range(LT):
                            last = nc.tensor.transpose(ptp[:, t, r * P:(r + 1) * P],
                                                       probs[:, r, t * P:(t + 1) * P], ident)
                    last.then_inc(s["pt_ready"], 1)

                def pv(b):
                    pe.wait_ge(s["ptl_ready"], ga.at(G, b + 1))
                    pe.wait_ge(s["ptt_ready"], ga.at(G, b + 1))
                    pe.wait_ge(s["nlo_ready"], ga.at(G, b + 1))
                    if b % (G // 2) == 0:
                        pe.wait_ge(tailc_in, ga.at(32, 16 * (b // (G // 2) + 1)))
                    if not (ph.which == "first" and b == 0):
                        pe.wait_ge(s["pcl_ready"], ga.at(G, b))
                    n = nat[b % 2]
                    terms = [(n[:, t, lo:lo + P], p_[:, t]) for t in range(LT)
                             for lo, p_ in ((0, pth), (0, ptl), (256, pth))]
                    terms.append((tailc[:, b % (G // 2), 0:P], ptt[:]))
                    for k, (w, x) in enumerate(terms):
                        mm(acc[:, 0], w, x, start=k == 0, stop=k == len(terms) - 1)
                    terms = [(n[:, t, P:2 * P], p_[:, t]) for t in range(LT) for p_ in (pth, ptl)]
                    terms.append((tailc[:, b % (G // 2), P:2 * P], ptt[:]))
                    for k, (w, x) in enumerate(terms):
                        last = mm(acc[:, 1], w, x, start=k == 0, stop=k == len(terms) - 1)
                    last.then_inc(s["acc_ready"], 1)

                def wv(p):
                    out_ = tile(f"WV{p}")
                    if p == 0:
                        pe.wait_ge(s["pcl_ready"], gp.at(G, G))
                    terms = [(w[:, c, h], x[:, c, h]) for h in (2 * p, 2 * p + 1) for c in range(2)
                             for w, x in ((wv_h, pc_h), (wv_l, pc_h), (wv_h, pc_l))]
                    for k, (w, x) in enumerate(terms):
                        last = mm(out_[:, 0], w, x, start=k == 0, stop=k == len(terms) - 1)
                    done(f"WV{p}", last)

                def y1():
                    out_ = tile("Y1")
                    drained("WV3")
                    for t in range(2):
                        t_ = slice(t * P, (t + 1) * P)
                        terms = [(o[:, p, t_], w[:, p]) for p in range(4)
                                 for o, w in ((oh, wo_h), (ol, wo_h), (oh, wo_l))]
                        for k, (w, x) in enumerate(terms):
                            last = mm(out_[:, t], w, x, start=k == 0, stop=k == len(terms) - 1)
                    done("Y1", last)

                def project(name):
                    w = {"z": wz, "k": w2[:, 0], "r": w2[:, 2]}[name]
                    out_ = tile(name)
                    drained("XT2")
                    for o in range(2):
                        for c in range(2):
                            last = mm(out_[:, o], w[:, c, o * P:(o + 1) * P], xt[:, c], start=c == 0,
                                      stop=c == 1)
                    done(name, last)

                def v():
                    out_ = tile("v")
                    for t in range(2):
                        for c in range(2):
                            last = mm(out_[:, t], xt[:, c, t * P:(t + 1) * P], w2[:, 1, c], start=c == 0,
                                      stop=c == 1)
                    done("v", last)

                def s_tile(j):
                    t, h = j // 4, j % 4
                    rows = slice(64 * (h % 2), 64 * (h % 2) + 64)
                    cols = slice((h // 2) * T + t * P, (h // 2) * T + t * P + P)
                    out_ = tile(f"S{j}")
                    if j == 0:
                        pe.wait_ge(s["rhat_ready"], gp.at(1, 1))
                        pe.wait_ge(s["khat_ready"], gp.at(1, 1))
                    for l in range(LEVELS):
                        last = mm(out_[:, l // 2, (l % 2) * P:(l % 2 + 1) * P], khat[rows, l, cols],
                                  rhat[rows, l, cols], start=True, stop=True)
                    done(f"S{j}", last)

                def o2_():
                    out_ = tile("O2")
                    drained("S7")
                    drained("v")
                    for j in range(8):
                        t, h = j // 4, j % 4
                        r0 = 64 * (h % 2)
                        last = mm(out_[r0:r0 + 64, h // 2, t * P:(t + 1) * P],
                                  vt[:, t, h * 64:(h + 1) * 64], s2[:, j], start=True, stop=True)
                    done("O2", last)

                def y2():
                    out_ = tile("Y2")
                    drained("O2")
                    for t in range(2):
                        for c in range(2):
                            last = mm(out_[:, t], o2[:, c, t * P:(t + 1) * P], wo2[:, c], start=c == 0,
                                      stop=c == 1)
                    done("Y2", last)

                def pf_():
                    out_ = tile("Pf")
                    drained("XT3")
                    for c in range(2):
                        last = mm(out_[0:R, 0], u1[:, c], xt[:, c], start=c == 0, stop=c == 1)
                    done("Pf", last)

                def hidden(i):
                    out_ = tile(f"H{i}")
                    drained("Pf")
                    for c in range(2):
                        f = (2 * i + c) * P
                        last = mm(out_[:, c], v1[:, f:f + P], pf, start=True, stop=True)
                    done(f"H{i}", last)

                def qf_(half):
                    out_ = tile("Qf") if half == 0 else gb[bank_of(ph, "Qf")]
                    for i in (2 * half, 2 * half + 1):
                        drained(f"H{i}")
                        for c in (2 * i, 2 * i + 1):
                            last = mm(out_[0:R, 0], u2[:, c], hid[:, c], start=c == 0, stop=c == 7)
                    if half:
                        done("Qf", last)

                def y3():
                    out_ = tile("Y3")
                    drained("Qf")
                    for t in range(2):
                        last = mm(out_[:, t], qf[:, t * P:(t + 1) * P], v2, start=True, stop=True)
                    done("Y3", last)

                steps = {"Y1": y1, "v": v, "O2": o2_, "Y2": y2, "Pf": pf_, "Y3": y3,
                         "hats": lambda: None}
                for n in ("XT", "XT2", "XT3"):
                    steps[n] = lambda n=n: turn(n)
                for n in "zkr":
                    steps[n] = lambda n=n: project(n)
                for i in range(8):
                    steps[f"Qk{i}"] = lambda i=i: qk(i)
                    steps[f"S{i}"] = lambda i=i: s_tile(i)
                for i in range(4):
                    steps[f"q{i}"] = lambda i=i: q(i)
                    steps[f"WV{i}"] = lambda i=i: wv(i)
                    steps[f"H{i}"] = lambda i=i: hidden(i)
                for i in range(2):
                    steps[f"Qf{i}"] = lambda i=i: qf_(i)

                for n in START:
                    if ph.has(n):
                        steps[n]()
                if ga:
                    score(0)
                for b in range(G):
                    if ga:
                        turn_probs(b)
                        if b + 1 < G:
                            score(b + 1)
                    if gp:
                        for n in FILL1[b]:
                            steps[n]()
                    if ga:
                        pv(b)
                    if gp:
                        for n in FILL2[b]:
                            steps[n]()

            turns(pe, body)

        @block.scalar
        def _(act):
            go = nc.scalar.activation

            def body(ph):
                ga, gp = ph.a, ph.b

                def wait_tile(name):
                    bank = bank_of(ph, name)
                    act.wait_ge(bank_filled[bank], filled(ph, name))
                    return gb[bank]

                def drain(name, last):
                    last.then_inc(bank_drained[bank_of(ph, name)], 1)

                def t_hi(b):
                    act.wait_ge(ctxt_in[b % 2], ga.at(16 * G // 2, 16 * (b // 2 + 1)))
                    if not (ph.which == "first" and b < 2):
                        act.wait_ge(s["scores_ready"], ga.at(2 * G, 2 * (b - 1)))
                    go(t0h[b % 2][:], raw_t[b % 2][:, 0], ACT.Copy)
                    if not (ph.which == "first" and b < 1):
                        act.wait_ge(s["tlo_ready"], ga.at(G, b))
                    go(t1s[64:128], raw_t[b % 2][64:128, 1], ACT.Copy).then_inc(s["thi_ready"], 1)

                def n_hi(b):
                    act.wait_ge(ctxn_in[b % 2], ga.at(16 * G // 2, 16 * (b // 2 + 1)))
                    if not (ph.which == "first" and b < 2):
                        act.wait_ge(s["acc_ready"], ga.at(G, b - 1))
                    go(nat[b % 2][:, :, 0:C], raw_n[b % 2][:], ACT.Copy).then_inc(s["nhi_ready"], 1)

                def exps(b):
                    for r in range(2):
                        act.wait_ge(s["nmax_ready"], ga.at(2 * G, 2 * b + r + 1))
                        go(probs[:, r, 0:L], scores[:, r, 0:L], ACT.Exp, bias=nmax[:, r:r + 1],
                           accum_out=rsum[:, r:r + 1]).then_inc(s["exp_ready"], 1)

                def pt_hi(b):
                    act.wait_ge(s["pt_ready"], ga.at(G, b + 1))
                    go(pth[:], ptp[:], ACT.Copy).then_inc(s["pth_ready"], 1)

                def pc_hi(b):
                    act.wait_ge(s["acc_ready"], ga.at(G, b + 1))
                    go(pc_h[:, :, :, b * S:(b + 1) * S], acc[:].rearrange("p c (h s) -> p c h s", h=H),
                       ACT.Copy).then_inc(s["pch_ready"], 1)

                def step(n):
                    if n in ("hats", "Y1", "Y2", "Y3", "Qf0") or n[0] == "S":
                        return
                    t = wait_tile("Qf" if n == "Qf1" else n)
                    if n == "XT":
                        go(xth[:], t[:], ACT.Copy).then_inc(s["xthi_ready"], 1)
                    elif n == "XT2":
                        for c in range(2):
                            last = go(xt[:, c], t[:, c], ACT.Identity, scale=vecs[:, c:c + 1],
                                      bias=vecs[:, 2 + c:3 + c])
                        drain(n, last)
                    elif n == "XT3":
                        drain(n, go(xt[:], t[:], ACT.Copy))
                    elif n[0] == "q":
                        p = int(n[1])
                        for i in range(2):
                            last = go(qs[0:64, (2 * p + i) % 4], t[64 * i:64 * i + 64, 0], ACT.Copy)
                        last.then_inc(s["qhi_ready"], 1)
                    elif n[:2] == "Qk":
                        h = int(n[2])
                        go(qk_h[:, :, :, h * S:(h + 1) * S],
                           t[:].rearrange("p c (b s) -> p c b s", b=G), ACT.Copy)\
                            .then_inc(s["qkhi_ready"], 1)
                    elif n[:2] == "WV":
                        go(oh[:, int(n[2])], t[:, 0], ACT.Copy).then_inc(s["oh_ready"], 1)
                    elif n == "z":
                        if ph.which == "last":
                            act.wait_ge(out_done, 16 * (NG - 1))
                        else:
                            act.wait_ge(out_done, gp.at(16, 0))
                        for c in range(2):
                            last = go(at[:, c], t[:, c], ACT.Tanh, scale=0.5, bias=vecs[:, 4 + c:5 + c])
                        drain(n, last)
                    elif n == "r":
                        drain(n, go(rt_[:], t[:], ACT.Tanh, scale=0.5))
                    elif n == "k":
                        drain(n, go(kt[:], t[:], ACT.Copy))
                    elif n == "v":
                        drain(n, go(vt[:], t[:], ACT.Copy))
                    elif n == "O2":
                        drain(n, go(o2, t[:], ACT.Copy))
                    elif n == "Pf":
                        drain(n, go(pf, t[0:R, 0], ACT.Copy))
                    elif n[0] == "H":
                        i = int(n[1])
                        for c in range(2):
                            f = 2 * i + c
                            last = go(hid[:, f], t[:, c], ACT.Gelu_apprx_tanh, bias=vecs[:, 6 + f:7 + f])
                        drain(n, last)
                    elif n == "Qf1":
                        drain("Qf", go(qf, t[0:R, 0], ACT.Copy))

                if ga:
                    t_hi(0)
                for n in START:
                    if ph.has(n):
                        step(n)
                    if n == "q1" and ga:
                        t_hi(1)
                        n_hi(0)
                if ga:
                    exps(0)
                for b in range(G):
                    if ga:
                        pt_hi(b)
                        if b + 1 < G:
                            exps(b + 1)
                    if gp:
                        for n in FILL1[b]:
                            step(n)
                    if ga:
                        if b + 2 < G:
                            t_hi(b + 2)
                        if b + 1 < G:
                            n_hi(b + 1)
                        pc_hi(b)
                    if gp:
                        for n in FILL2[b]:
                            step(n)
                if gp:
                    act.wait_ge(bank_drained[bank_of(ph, "Y3")], filled(ph, "Y3"))
                    act.dma_start(out_v[gp.index], ob[:]).then_inc(out_done, 16)

            act.wait_ge(s["weights_ready"], 1)
            turns(act, body)
            act.wait_ge(out_done, 16 * NG)

        @block.vector
        def _(dve):
            v_ = nc.vector
            chain = Chain(dve, s["dve_chain"], *DVE_LINKS)
            chain.k, chain.base = 0, 0
            link = chain.link

            for buf in (tailp[:].bitcast(F32), s2[:], tail3[:].bitcast(F32)):
                v_.memset(buf, 0.0)
            v_.memset(vecs[:, 14:16], -0.5)
            v_.memset(eps2[:], EPS)
            v_.memset(probs[:], 0.0)
            v_.memset(t1s[0:64].bitcast(F32), 0.0)
            link(v_.memset(fw[:], 1.0))
            dve.wait_ge(w_in, W_ALL)
            link(v_.tensor_copy(tail3[:, 0, 0:C], tail_raw[:]))
            v_.tensor_copy(tail3[:, 2, 0:C], tail_raw[:])
            v_.tensor_tensor(tail3[:, 1, 0:P], tail_raw[:, 0:P], tail3[:, 0, 0:P].bitcast(F32), ALU.subtract)
            for i in (0, 2):
                last = v_.tensor_tensor(tail3[:, i, C:256], tail_raw[:, P:C], tail3[:, 0, P:C].bitcast(F32),
                                        ALU.subtract)
            last.then_inc(s["tail_split"], 1)
            v_.tensor_copy(ident_r[:], ident_raw[:])
            v_.tensor_copy(mask[:], mask_raw[:])
            v_.tensor_scalar(vecs[:, 4:6], bw_raw[:], 0.5, None, ALU.mult)
            v_.tensor_copy(wq_h[:], wq_raw[:])
            v_.tensor_copy(wo_h[:], wo_raw[:])
            v_.tensor_copy(wv_h[:], wv_raw[:])
            link(v_.tensor_scalar(wk_h[:], wk_raw[:], SCALE, None, ALU.mult))
            v_.tensor_tensor(wq_l[:], wq_raw[:], wq_h[:].bitcast(F32), ALU.subtract)
            v_.tensor_tensor(wo_l[:], wo_raw[:], wo_h[:].bitcast(F32), ALU.subtract)
            v_.tensor_tensor(wv_l[:], wv_raw[:], wv_h[:].bitcast(F32), ALU.subtract)
            v_.scalar_tensor_tensor(wk_l[:], wk_raw[:], SCALE, wk_h[:].bitcast(F32), ALU.mult, ALU.subtract)
            dve.wait_ge(s["wz_psum"], 1)
            v_.tensor_copy(wz[:], gb[0][:]).then_inc(s["weights_ready"], 1)
            setup_links = chain.k

            def body(ph):
                ga, gp = ph.a, ph.b
                chain.begin(ph, setup_links)
                held = []

                def wait_tile(name):
                    bank = bank_of(ph, name)
                    dve.wait_ge(bank_filled[bank], filled(ph, name))
                    return gb[bank]

                def drain(name, last):
                    last.then_inc(bank_drained[bank_of(ph, name)], 1)

                def own_drain(name):
                    dve.wait_ge(bank_drained[bank_of(ph, name)], filled(ph, name))

                def norm(x, ln):
                    v_.bn_stats(stats[:, 0], x[:, 0])
                    link(v_.bn_stats(stats[:, 1], x[:, 1]))
                    hold()
                    for t in range(2):
                        last = v_.bn_aggr(mv[:, ln, t], stats[:, t])
                    link(last)
                    v_.tensor_scalar(ve[:, ln], mv[:, ln, :, 1], EPS, None, ALU.add)\
                        .then_inc(s["var_ready"], 1)
                    dve.wait_ge(s["rstd_ready"], xn_count(ph, ln))
                    k = 3 if ln == 1 else ln
                    for t in range(2):
                        last = v_.tensor_scalar(xn[:, t], x[:, t], mv[:, ln, t, 0:1], rstd[:, k, t:t + 1],
                                                ALU.subtract, ALU.mult)
                    last.then_inc(s["xn_ready"], 1)

                def hold():
                    if held:
                        dve.wait_ge(chain.sem, chain.base + held[-1])
                    v_.memset(cell[:], 0.0).then_inc(chain.sem, 1)
                    chain.k += 1
                    held.append(chain.k)

                def nmaxs(b):
                    for r in range(2):
                        dve.wait_ge(s["scores_ready"], ga.at(2 * G, 2 * b + r + 1))
                        v_.tensor_reduce(nmax[:, r:r + 1], scores[:, r, 0:L], AX.X, ALU.max, negate=True)\
                            .then_inc(s["nmax_ready"], 1)

                def norm_probs(b):
                    dve.wait_ge(s["exp_ready"], ga.at(2 * G, 2 * b + 2))
                    link(v_.reciprocal(rinv[:], rsum[:]))
                    for r in range(2):
                        last = v_.tensor_scalar(probs[:, r, 0:L], probs[:, r, 0:L], rinv[:, r:r + 1], None,
                                                ALU.mult)
                    link(last)
                    for i in range(2):
                        last = v_.tensor_copy(tailp[:, :, i:i + 1], probs[:, :, L - 1:L])
                    link(last)
                    v_.tensor_tensor(tailp[:, :, 2:3], probs[:, :, L - 1:L], tailp[:, :, 0:1].bitcast(F32),
                                     ALU.subtract).then_inc(s["probs_ready"], 1)

                def tail_out(b):
                    dve.wait_ge(s["tailt_ready"], ga.at(G, b + 1))
                    v_.tensor_copy(ptt[:].rearrange("a (r q) -> a r q", r=2), scores[0:3, :, 384:512])\
                        .then_inc(s["ptt_ready"], 1)

                def pt_lo(b):
                    dve.wait_ge(s["pth_ready"], ga.at(G, b + 1))
                    v_.tensor_tensor(ptl[:], ptp[:], pth[:].bitcast(F32), ALU.subtract)\
                        .then_inc(s["ptl_ready"], 1)

                def pc_lo(b):
                    dve.wait_ge(s["pch_ready"], ga.at(G, b + 1))
                    b_ = slice(b * S, (b + 1) * S)
                    v_.tensor_tensor(pc_l[:, :, :, b_], acc[:].rearrange("p c (h s) -> p c h s", h=H),
                                     pc_h[:, :, :, b_].bitcast(F32), ALU.subtract)\
                        .then_inc(s["pcl_ready"], 1)

                def decays():
                    own_wait = bank_drained[bank_of(ph, "z")]
                    dve.wait_ge(own_wait, filled(ph, "z"))
                    a_flat = at[:].rearrange("p c t -> p (c t)")
                    a4, f4 = a_flat.rearrange("p (n i) -> p n i", i=4), fw[:].rearrange("p (n i) -> p n i", i=4)
                    link(v_.tensor_scalar(a_flat, a_flat, -0.5, 0.5, ALU.mult, ALU.add))
                    link(v_.tensor_scalar(f4[:, :, 1:2], a4[:, :, 1:2], A_MIN, None, ALU.max))
                    for i in (2, 3):
                        link(v_.scalar_tensor_tensor(f4[:, :, i:i + 1], a4[:, :, i:i + 1], A_MIN,
                                                     f4[:, :, i - 1:i], ALU.max, ALU.mult))
                    link(v_.reciprocal(bw_[:], fw[:]))
                    link(v_.scalar_tensor_tensor(pw[:].rearrange("p (n i) -> p n i", i=4),
                                                 a4[:, :, 0:1].to_broadcast([P, T // 2, 4]), A_MIN, f4,
                                                 ALU.max, ALU.mult))
                    k_flat = kt[:].rearrange("p c t -> p (c t)")
                    dve.wait_ge(bank_drained[bank_of(ph, "k")], filled(ph, "k"))
                    wait_tile("v")
                    v_.tensor_tensor(khat[:, 0], k_flat, bw_[:], ALU.mult)
                    dve.wait_ge(bank_drained[bank_of(ph, "r")], filled(ph, "r"))
                    link(v_.tensor_scalar(rt_[:], rt_[:], 0.5, 0.5, ALU.mult, ALU.add))
                    r_flat = rt_[:].rearrange("p c t -> p (c t)")
                    v_.tensor_tensor(rhat[:, 0], r_flat, fw[:], ALU.mult)
                    link(v_.tensor_tensor(bw_[:].rearrange("p (n i) -> p n i", i=4),
                                          bw_[:].rearrange("p (n i) -> p n i", i=4),
                                          f4[:, :, 3:4].to_broadcast([P, T // 2, 4]), ALU.mult))

                def hats():
                    k_flat = kt[:].rearrange("p c t -> p (c t)")
                    r_flat = rt_[:].rearrange("p c t -> p (c t)")
                    for l in range(1, LEVELS):
                        n = 2 << l

                        def two(x):
                            return x.rearrange("p (m h i) -> p m h i", h=2, i=n)

                        blocks = 2 * T // (2 * n)
                        last = v_.tensor_tensor(khat[:, l], k_flat, bw_[:], ALU.mult)
                        last2 = v_.tensor_tensor(rhat[:, l], r_flat, pw[:], ALU.mult)
                        if l == LEVELS - 1:
                            last.then_inc(s["khat_ready"], 1)
                            last2.then_inc(s["rhat_ready"], 1)
                        else:
                            link(last2)
                            link(v_.tensor_tensor(two(bw_[:])[:, :, 0], two(bw_[:])[:, :, 0],
                                                  two(pw[:])[:, :, 1, n - 1:n].to_broadcast([P, blocks, n]),
                                                  ALU.mult))
                            link(v_.tensor_tensor(two(pw[:])[:, :, 1], two(pw[:])[:, :, 1],
                                                  two(pw[:])[:, :, 0, n - 1:n].to_broadcast([P, blocks, n]),
                                                  ALU.mult))

                def step(n):
                    if n == "XT":
                        t = wait_tile(n)
                        dve.wait_ge(s["xthi_ready"], ga.at(1, 1))
                        drain(n, v_.tensor_tensor(xtl[:], t[:], xth[:].bitcast(F32), ALU.subtract))
                    elif n[0] == "q":
                        p = int(n[1])
                        t = wait_tile(n)
                        dve.wait_ge(s["qhi_ready"], ga.at(4, p + 1))
                        for i in range(2):
                            h = (2 * p + i) % 4
                            last = v_.tensor_tensor(qs[64:128, h], t[64 * i:64 * i + 64, 0],
                                                    qs[0:64, h].bitcast(F32), ALU.subtract)
                        drain(n, last)
                    elif n[:2] == "Qk":
                        h = int(n[2])
                        t = wait_tile(n)
                        dve.wait_ge(s["qkhi_ready"], ga.at(H, h + 1))
                        h_ = slice(h * S, (h + 1) * S)
                        drain(n, v_.tensor_tensor(qk_l[:, :, :, h_], t[:].rearrange("p c (b s) -> p c b s", b=G),
                                                  qk_h[:, :, :, h_].bitcast(F32), ALU.subtract))
                    elif n[:2] == "WV":
                        p = int(n[2])
                        t = wait_tile(n)
                        dve.wait_ge(s["oh_ready"], gp.at(4, p + 1))
                        drain(n, v_.tensor_tensor(ol[:, p], t[:, 0], oh[:, p].bitcast(F32), ALU.subtract))
                    elif n == "Y1":
                        dve.wait_ge(s["xb_ready"], gp.at(1, 1))
                        drain(n, v_.tensor_tensor(x12[:], wait_tile(n)[:], xb[:], ALU.add))
                        own_drain(n)
                        norm(x12, 1)
                    elif n == "z":
                        pass
                    elif n == "v":
                        decays()
                    elif n == "hats":
                        hats()
                    elif n[0] == "S":
                        j = int(n[1])
                        t = wait_tile(n)
                        for l in range(LEVELS):
                            hold()
                            i = v_.copy_predicated(s2[:, j], mask[:, l], t[:, l // 2, (l % 2) * P:(l % 2 + 1) * P])
                            if l < LEVELS - 1:
                                link(i)
                        drain(n, i)
                    elif n == "Y2":
                        drain(n, v_.tensor_tensor(x12[:], wait_tile(n)[:], x12[:], ALU.add))
                        own_drain(n)
                        norm(x12, 2)
                    elif n == "Y3":
                        t = wait_tile(n)
                        dve.wait_ge(s["ob_ready"], gp.at(1, 1))
                        drain(n, v_.tensor_tensor(ob[:], t[:], ob[:], ALU.add))

                if ga:
                    dve.wait_ge(x_in, ga.at(16, 16))
                    norm(xin, 0)
                for n in START:
                    if ph.has(n):
                        step(n)
                if ga:
                    nmaxs(0)
                    norm_probs(0)
                for b in range(G):
                    if ga:
                        tail_out(b)
                        pt_lo(b)
                        if b + 1 < G:
                            nmaxs(b + 1)
                    if gp:
                        for n in FILL1[b]:
                            step(n)
                    if ga:
                        if b + 1 < G:
                            norm_probs(b + 1)
                        pc_lo(b)
                    if gp:
                        for n in FILL2[b]:
                            step(n)
                if ph.which != "last":
                    assert chain.k == DVE_LINKS[ph.which == "middle"], chain.k

            turns(dve, body)

        @block.gpsimd
        def _(pool):
            p_ = nc.gpsimd
            chain = Chain(pool, s["pool_chain"], *POOL_LINKS)

            def body(ph):
                ga, gp = ph.a, ph.b
                chain.begin(ph, 0)
                link = chain.link
                half = vecs[:, 14:16]

                def t_lo(b):
                    pool.wait_ge(s["thi_ready"], ga.at(G, b + 1))
                    i = b % 2
                    p_.tensor_tensor(t0l[i][:], raw_t[i][:, 0], t0h[i][:].bitcast(F32), ALU.subtract)
                    p_.tensor_tensor(t1[i][:], raw_t[i][:, 1], t1s[:].bitcast(F32), ALU.subtract)\
                        .then_inc(s["tlo_ready"], 1)

                def n_lo(b):
                    pool.wait_ge(s["nhi_ready"], ga.at(G, b + 1))
                    i = b % 2
                    p_.tensor_tensor(nat[i][:, :, 256:384], raw_n[i][:, :, 0:P],
                                     nat[i][:, :, 0:P].bitcast(F32), ALU.subtract)
                    p_.tensor_tensor(nat[i][:, :, C:256], raw_n[i][:, :, P:C],
                                     nat[i][:, :, P:C].bitcast(F32), ALU.subtract)\
                        .then_inc(s["nlo_ready"], 1)

                def rstds(ln):
                    pool.wait_ge(s["var_ready"], xn_count(ph, ln))
                    i = p_.tensor_tensor(rstd[:, ln], ve[:, ln], half, ALU.pow)
                    if ln == 1:
                        link(i)
                        link(p_.tensor_tensor(rstd[:, 3], mv[:, 1, :, 1], rstd[:, 1], ALU.mult))
                        link(p_.tensor_tensor(rstd[:, 3], rstd[:, 3], rstd[:, 1], ALU.mult))
                        link(p_.tensor_tensor(rstd[:, 3], rstd[:, 3], eps2[:], ALU.add))
                        link(p_.tensor_tensor(rstd[:, 3], rstd[:, 3], half, ALU.pow))
                        i = p_.tensor_tensor(rstd[:, 3], rstd[:, 3], rstd[:, 1], ALU.mult)
                    i.then_inc(s["rstd_ready"], 1)

                if ga:
                    rstds(0)
                    t_lo(0)
                    t_lo(1)
                    n_lo(0)
                if gp:
                    rstds(1)
                if ga:
                    if gp:
                        pool.wait_ge(bank_drained[bank_of(ph, "Y1")], filled(ph, "Y1"))
                    pool.wait_ge(s["xn_ready"], xn_count(ph, 0))
                    p_.tensor_tensor(xb[:], xin[:], bo[:].rearrange("p (o d) -> p o d", o=1).to_broadcast([P, 2, D]),
                                     ALU.add).then_inc(s["xb_ready"], 1)
                for b in range(G):
                    if ga:
                        if b + 2 < G:
                            t_lo(b + 2)
                        if b + 1 < G:
                            n_lo(b + 1)
                    if gp and b == 6:
                        rstds(2)
                        pool.wait_ge(s["khat_ready"], gp.at(1, 1))
                        p_.tensor_tensor(ob[:], x12[:], b2[:].rearrange("p (o d) -> p o d", o=1).to_broadcast([P, 2, D]),
                                         ALU.add).then_inc(s["ob_ready"], 1)
                if ph.which != "last":
                    assert chain.k == POOL_LINKS[ph.which == "middle"], chain.k

            pool.wait_ge(s["weights_ready"], 1)
            turns(pool, body)


def xn_count(phase, ln):
    if phase.which == "first":
        return 1
    if phase.which == "middle":
        return phase.m * 3 + (2 + ln)
    return 1 + 3 * (NG - 1) + ln


def level_masks():
    t = np.arange(P)
    key, query = t[:, None], t[None, :]
    masks = [(key // 4 == query // 4) & (key <= query)]
    for n in (4, 8, 16):
        masks.append((key // (2 * n) == query // (2 * n)) & (key // n < query // n))
    return np.stack(masks, 1).astype(np.float32)


def chunks(w, p=P):
    return np.ascontiguousarray(w.reshape(-1, p, w.shape[-1]).transpose(1, 0, 2))


def kernel(x, ctx_768, L0_xattn_Wq, L0_xattn_Wk, L0_xattn_Wv, L0_xattn_Wo, L0_xattn_bo, L0_attn_ln_g,
           L0_attn_ln_b, L0_attn_Wx, L0_attn_Ww, L0_attn_bw, L0_attn_Wk, L0_attn_Wv, L0_attn_Wr,
           L0_attn_Wo, L0_ffn_U1, L0_ffn_V1, L0_ffn_b1, L0_ffn_U2, L0_ffn_V2, L0_ffn_b2):
    import concourse.bacc as bacc
    from concourse.bass_utils import run_bass_kernel_spmd

    c = np.asarray(ctx_768)
    ctx_t = np.zeros((B, P, 2, LP), c.dtype)
    ct = c.transpose(0, 2, 1)
    ctx_t[:, :, 0, :L] = ct[:, :P]
    ctx_t[:, :64, 1, :L] = ct[:, P:]
    ctx_t[:, 64:, 1, :L] = ct[:, P:]
    ctx_n = np.ascontiguousarray(c[:, :LT * P].reshape(B, LT, P, C).transpose(0, 2, 1, 3))
    wk = np.asarray(L0_xattn_Wk).T.reshape(H, DH, C).transpose(1, 0, 2)
    wk = np.concatenate([wk, wk[:, :, P:]], 2)
    wk = np.concatenate([wk, wk], 0)
    wv_ = np.asarray(L0_xattn_Wv)
    wv = np.zeros((P, 2, H, P), wv_.dtype)
    for h in range(H):
        o = 64 * (h % 2)
        wv[:, 0, h, o:o + 64] = wv_[:P, h * 64:(h + 1) * 64]
        wv[:64, 1, h, o:o + 64] = wv_[P:, h * 64:(h + 1) * 64]
        wv[64:, 1, h, o:o + 64] = wv_[P:, h * 64:(h + 1) * 64]

    def column(v):
        return np.ascontiguousarray(np.asarray(v).reshape(-1, P).T)

    def rows(v):
        return np.ascontiguousarray(np.broadcast_to(np.asarray(v), (P, D)))

    arrays = {
        "x": np.ascontiguousarray(np.asarray(x).reshape(B * S, D)), "ctx_t": ctx_t, "ctx_n": ctx_n,
        "ctx_tail": np.ascontiguousarray(c[:, L - 1]),
        "wq": chunks(np.asarray(L0_xattn_Wq)), "wk": wk, "wv": wv, "wo": chunks(np.asarray(L0_xattn_Wo)),
        "bo": rows(L0_xattn_bo), "ln_g": column(L0_attn_ln_g), "ln_b": column(L0_attn_ln_b),
        "wxt": chunks(np.asarray(L0_attn_Wx).T), "ww": chunks(np.asarray(L0_attn_Ww)),
        "bw": column(L0_attn_bw), "wk2": chunks(np.asarray(L0_attn_Wk)),
        "wv2": chunks(np.asarray(L0_attn_Wv)), "wr2": chunks(np.asarray(L0_attn_Wr)),
        "wo2": chunks(np.asarray(L0_attn_Wo)), "u1": chunks(np.asarray(L0_ffn_U1)),
        "v1": np.asarray(L0_ffn_V1), "b1": column(L0_ffn_b1), "u2": chunks(np.asarray(L0_ffn_U2)),
        "v2": np.asarray(L0_ffn_V2), "b2": rows(L0_ffn_b2),
        "ident": np.eye(P, dtype=np.float32), "mask": level_masks(),
    }
    nc = bacc.Bacc("TRN2", target_bir_lowering=False, num_devices=1)
    a = {n: nc.dram_tensor(f"in_{n}", v.shape, mybir.dt.from_np(v.dtype), kind="ExternalInput").ap()
         for n, v in arrays.items()}
    out = nc.dram_tensor("out", (B * S, D), F32, kind="ExternalOutput").ap()
    build(nc, a, out)
    r = run_bass_kernel_spmd(nc, [{f"in_{n}": v for n, v in arrays.items()}], core_ids=[0])
    return r.results[0]["out"].reshape(B, S, D)
```

```python
from contextlib import ExitStack

import concourse.bass as bass
import concourse.mybir as mybir
import numpy as np

F32 = mybir.dt.float32
F32R = mybir.dt.float32r
U8 = mybir.dt.uint8
ACT = mybir.ActivationFunctionType
ALU = mybir.AluOpType
AX = mybir.AxisListType

B, S, D = 128, 32, 256
L, C = 257, 192
H, DH = 8, 64
INNER = H * DH
F, R = 1024, 64
G = 8
NG = B // G
T = G * S
P = 128
LP = L + 1
LT = 2
SCALE = DH ** -0.5
EPS = 1e-5
A_MIN = 2.0 ** -25
LEVELS = 4

START = ["WV0", "WV1", "XT3", "WV2", "XT", "Pf", "WV3", "q0", "H0", "q1", "H1", "Qk0", "Qk1", "Y1", "q2",
         "H2", "Qk2", "Qk3", "q3", "H3", "Qk4", "Qk5", "Qk6", "Qk7", "XT2"]
AFTER_SCORE = ["Qf"]
FILL1 = [["z"], ["Y3"], ["v"], ["Sa0"], ["Sa2", "Sa3"], ["Sb1", "Sb2"], ["O2"], ["Y2"]]
FILL2 = [["k"], ["r"], [], ["Sa1"], ["Sb0"], ["Sb3"], [], []]
GAPS = [[[], [], [], ["f1"]],
        [["i1"], ["f2", "i2"], ["f3", "Y3"], ["i3"]],
        [["pw"], ["bw"], ["k1"], ["b1"]],
        [["p1"], ["k2"], ["b2", "Sa0"], ["p2"]],
        [["Sa1"], ["k3", "Sa2"], ["Sa3"], []],
        [["Sb0"], ["Sb1"], ["Sb2"], []],
        [["Sb3"], [], [], []],
        [[], [], [], ["Y2"]]]
GAP_STEPS = {n for gaps in GAPS for gap in gaps for n in gap if n[0] in "fipbk"}
A_STEPS = {"XT"} | {f"q{p}" for p in range(4)} | {f"Qk{h}" for h in range(H)}
C_STEPS = {f"H{i}" for i in range(4)} | {"XT3", "Pf", "Qf", "Y3"}
BANK_ORDER = START + AFTER_SCORE + [n for b in range(G) for n in FILL1[b] + FILL2[b]]
BANKS = 4


class Group:

    def __init__(self, register, plus):
        self.register, self.plus = register, plus
        self.index = register + plus

    def at(self, per_group, k):
        return self.register * per_group + (self.plus * per_group + k)


class Phase:

    def __init__(self, which, m):
        self.which, self.m = which, m
        self.a, self.b, self.c = {
            "a": (Group(0, 0), None, None), "ab": (Group(0, 1), Group(0, 0), None),
            "abc": (Group(m, 2), Group(m, 1), Group(m, 0)),
            "bc": (None, Group(0, NG - 1), Group(0, NG - 2)), "c": (None, None, Group(0, NG - 1))}[which]

    def group_of(self, name):
        return self.a if name in A_STEPS else self.c if name in C_STEPS else self.b

    def has(self, name):
        return self.group_of(name) is not None

    def before(self, count):
        total = 0
        for which in ("a", "ab", "abc", "bc"):
            if which == self.which:
                return total if which != "abc" else self.m * count(which) + total
            total += count(which) * (NG - 2 if which == "abc" else 1)
        return total


def order_of(which):
    phase = Phase(which, 0)
    return [n for n in BANK_ORDER if phase.has(n)]


def bank_of(phase, name):
    return order_of(phase.which).index(name) % BANKS


def filled(phase, name, k=1):
    bank = bank_of(phase, name)
    here = order_of(phase.which).index(name) // BANKS + k
    return phase.before(lambda which: len(order_of(which)[bank::BANKS])) + here


class Chain:

    def __init__(self, engine, sem, setup, counts):
        self.engine, self.sem, self.setup, self.counts = engine, sem, setup, counts
        self.k, self.base = 0, 0

    def begin(self, phase):
        self.k = 0
        self.base = phase.before(lambda which: self.counts[which]) + self.setup

    def sign(self, instruction):
        instruction.then_inc(self.sem, 1)
        self.k += 1
        return self.k

    def need(self, k):
        self.engine.wait_ge(self.sem, self.base + k)

    def link(self, instruction):
        self.need(self.sign(instruction))


DVE_SETUP = 3
DVE_LINKS = {"a": 19, "ab": 54, "abc": 54, "bc": 35, "c": 0}
POOL_LINKS = {"a": 0, "ab": 5, "abc": 5, "bc": 5}


def build(nc, a, out):
    with ExitStack() as ctx:
        def sb(name, shape, dt=F32):
            return ctx.enter_context(nc.sbuf_tensor(name, shape, dt))

        def ps(name, shape):
            return ctx.enter_context(nc.psum_tensor(name, shape, F32))

        def sem(name):
            return ctx.enter_context(nc.semaphore(name))

        wq_h, wq_l = sb("wq_h", [P, 2, INNER], F32R), sb("wq_l", [P, 2, INNER], F32R)
        wk_h, wk_l = sb("wk_h", [P, H, 256], F32R), sb("wk_l", [P, H, 256], F32R)
        wv_h, wv_l = sb("wv_h", [P, 2, H, P], F32R), sb("wv_l", [P, 2, H, P], F32R)
        wo_h, wo_l = sb("wo_h", [P, 4, D], F32R), sb("wo_l", [P, 4, D], F32R)
        w2 = sb("w2", [P, 3, 2, D])
        wz = sb("wz", [P, 2, D])
        wo2 = sb("wo2", [P, 2, D])
        u1, u2 = sb("u1", [P, 2, R]), sb("u2", [P, 8, R])
        v12 = sb("v12", [P, F])
        v1, v2 = v12[0:R], v12[R:2 * R, 0:D]
        bo, b2 = sb("bo", [P, D]), sb("b2", [P, D])
        vecs = sb("vecs", [P, 16])
        ident_r = sb("ident_r", [P, P], F32R)
        ident = ident_r[:].bitcast(F32)
        mask = sb("mask", [P, LEVELS, P], U8)

        raw_t = [sb(f"raw_t{i}", [P, 2, LP]) for i in range(2)]
        raw_n = [sb(f"raw_n{i}", [P, LT, C]) for i in range(2)]
        t0h = [sb(f"t0h{i}", [P, LP], F32R) for i in range(2)]
        t0l = [sb(f"t0l{i}", [P, LP], F32R) for i in range(2)]
        t1 = [sb(f"t1_{i}", [P, LP], F32R) for i in range(2)]
        t1s = sb("t1s", [P, LP], F32R)
        nat = [sb(f"nat{i}", [P, LT, 384], F32R) for i in range(2)]
        probs = sb("probs", [P, 2, LP])
        tailp = sb("tailp", [P, 2, P], F32R)
        pth, ptl = sb("pth", [P, LT, 256], F32R), sb("ptl", [P, LT, 256], F32R)
        ptt = sb("ptt", [3, 256], F32R)
        nmax, rsum, rinv = sb("nmax", [P, 2]), sb("rsum", [P, 2]), sb("rinv", [P, 2])

        cell, eps2 = sb("cell", [1, 1]), sb("eps2", [P, 2])

        tailc = sb("tailc", [3, G // 2, 256], F32R)
        xin, xb, x12 = (sb(n, [P, 2, D]) for n in ("xin", "xb", "x12"))
        xn = sb("xn", [P, 2, D])
        stats, mv = sb("stats", [P, 2, 6]), sb("mv", [P, 3, 2, 2])
        ve, rstd = sb("ve", [P, 3, 2]), sb("rstd", [P, 4, 2])
        at, vt = sb("at", [P, 2, T]), sb("vt", [P, 2, T])
        fw = sb("fw", [P, 2 * T])
        ob = vt
        s2 = sb("s2", [P, 8, P])
        pq = sb("pq", [P, T])
        pf, qf = pq[0:R], pq[R:2 * R]

        KB = 1024
        base = (nc.sbuf_usable_end - 88 * KB) // 32 * 32
        assert nc.sbuf_base <= base, (nc.sbuf_base, base)

        def at_(name, shape, dt, offset):
            return nc.alloc_sbuf_tensor_at(name, shape, dt, offset=base + offset)

        hid = at_("hid", [P, 8, T], F32, 0)
        oh = at_("oh", [P, 4, T], F32R, 8 * KB)
        ol = at_("ol", [P, 4, T], F32R, 12 * KB)
        rhat = at_("rhat", [P, LEVELS, 2 * T], F32, 0)
        khat = at_("khat", [P, LEVELS, 2 * T], F32, 8 * KB)
        xt = at_("xt", [P, 2, T], F32, 14 * KB)
        xt3 = at_("xt3", [P, 2, T], F32, 6 * KB)
        xth = at_("xth", [P, 2, T], F32R, 80 * KB)
        xtl = at_("xtl", [P, 2, T], F32R, 82 * KB)
        qs = at_("qs", [P, 4, T], F32R, 84 * KB)
        kt = at_("kt", [P, 2, T], F32, 80 * KB)
        rt_ = at_("rt", [P, 2, T], F32, 82 * KB)
        bw_ = at_("bwd", [P, 2 * T], F32, 84 * KB)
        pw = at_("pw", [P, 2 * T], F32, 86 * KB)
        o2 = pw[:].rearrange("p (c t) -> p c t", c=2)

        qk_h = at_("qk_h", [P, 2, G, 256], F32R, 16 * KB)
        qk_l = at_("qk_l", [P, 2, G, 256], F32R, 32 * KB)
        pc_h = at_("pc_h", [P, 2, H, T], F32R, 48 * KB)
        pc_l = at_("pc_l", [P, 2, H, T], F32R, 64 * KB)
        scores = ps("scores", [P, 2, 512])
        ptp = ps("ptp", [P, LT, 256])
        acc = ps("acc", [P, 2, 256])
        gb = [ps(f"gb{i}", [P, 2, 256]) for i in range(BANKS)]

        w_in, x_in, tailc_in, out_done, scratch_in = (sem(n) for n in
                                                      ("w_in", "x_in", "tailc_in", "out_done", "scratch_in"))
        ctxt_in = [sem(f"ctxt_in{i}") for i in range(2)]
        ctxn_in = [sem(f"ctxn_in{i}") for i in range(2)]
        bank_filled = [sem(f"bank_filled{i}") for i in range(BANKS)]
        bank_drained = [sem(f"bank_drained{i}") for i in range(BANKS)]
        names = ("weights_ready wz_psum tail_split thi_ready tlo_ready nhi_ready nlo_ready "
                 "scores_ready nmax_ready exp_ready probs_ready tailp_ready tailt_ready ptt_ready pt_ready "
                 "pth_ready ptl_ready acc_ready pch_ready pcl_ready xthi_ready qhi_ready qkhi_ready "
                 "oh_ready xb_ready ob_ready var_ready rstd_ready xn_ready tanh_ready f_ready "
                 "inv_ready pw_ready hatp_ready hatv_ready dve_chain pool_chain").split()
        s = {n: sem(n) for n in names}

        x_v = a["x"].rearrange("(g t p) d -> g p t d", g=NG, p=P)
        out_v = out.rearrange("(g t p) d -> g p t d", g=NG, p=P)
        ctxt_v, ctxn_v = a["ctx_t"], a["ctx_n"]
        scratch = nc.dram_tensor("tail_scratch", [3, B, 256], F32, kind="Internal").ap()

        wq_raw = at_("wq_raw", [P, 2, INNER], F32, 16 * KB)
        wo_raw = at_("wo_raw", [P, 4, D], F32, 20 * KB)
        wk_raw = at_("wk_raw", [P, H, 256], F32, 24 * KB)
        wv_raw = at_("wv_raw", [P, 2, H, P], F32, 32 * KB)
        wxt_raw = at_("wxt_raw", [P, 2, D], F32, 40 * KB)
        ww_raw = at_("ww_raw", [P, 2, D], F32, 42 * KB)
        tail_raw = at_("tail_raw", [P, C], F32, 44 * KB)
        tail3 = at_("tail3", [P, 3, 256], F32R, 48 * KB)
        bw_raw = at_("bw_raw", [P, 2], F32, 52 * KB)
        ident_raw = at_("ident_raw", [P, P], F32, 53 * KB)
        mask_raw = at_("mask_raw", [P, LEVELS, P], F32, 54 * KB)

        LOADS = [(wq_raw[:], a["wq"]), (wo_raw[:], a["wo"]), (wk_raw[:], a["wk"]), (wv_raw[:], a["wv"]),
                 (wxt_raw[:], a["wxt"]), (ww_raw[:], a["ww"]), (tail_raw[:], a["ctx_tail"]),
                 (w2[:, 0], a["wk2"]), (w2[:, 1], a["wv2"]), (w2[:, 2], a["wr2"]), (wo2[:], a["wo2"]),
                 (u1[:], a["u1"]), (v1, a["v1"]), (u2[:], a["u2"]), (v2, a["v2"]),
                 (bo[:], a["bo"]), (b2[:], a["b2"]), (vecs[:, 0:2], a["ln_g"]), (vecs[:, 2:4], a["ln_b"]),
                 (bw_raw[:], a["bw"]), (vecs[:, 6:14], a["b1"]), (ident_raw[:], a["ident"]),
                 (mask_raw[:], a["mask"])]
        W_ALL = 16 * len(LOADS)

        block = ctx.enter_context(nc.Block())

        def turns(engine, body):
            body(Phase("a", 0))
            body(Phase("ab", 0))
            with engine.Fori(0, NG - 2) as m:
                body(Phase("abc", m))
            body(Phase("bc", 0))
            body(Phase("c", 0))

        @block.sync
        def _(sp):
            for dst, src in LOADS:
                sp.dma_start(dst, src).then_inc(w_in, 16)
            sp.wait_ge(s["tail_split"], 1)
            sp.dma_start(scratch.rearrange("r b c -> b r c"), tail3[:].bitcast(F32)).then_inc(scratch_in, 16)
            sp.wait_ge(scratch_in, 16)

            def body(ph):
                g = ph.a
                first = ph.which == "a"

                def load_t(b):
                    if not (first and b < 2):
                        sp.wait_ge(s["tlo_ready"], g.at(G, b - 1))
                    sp.dma_start(raw_t[b % 2][:], ctxt_v[g.index * G + b]).then_inc(ctxt_in[b % 2], 16)

                def load_n(b):
                    if not (first and b < 2):
                        sp.wait_ge(s["nlo_ready"], g.at(G, b - 1))
                    sp.dma_start(raw_n[b % 2][:], ctxn_v[g.index * G + b]).then_inc(ctxn_in[b % 2], 16)

                if not first:
                    sp.wait_ge(s["xb_ready"], g.at(1, 0))
                sp.dma_start(xin[:], x_v[g.index]).then_inc(x_in, 16)
                load_t(0)
                load_t(1)
                load_n(0)
                load_n(1)
                if not first:
                    sp.wait_ge(s["acc_ready"], g.at(G, 0))
                half = G // 2
                sp.dma_start(tailc[:].bitcast(F32), scratch[:, bass.ds(g.index * G, half)]).then_inc(tailc_in, 16)
                for b in range(2, G):
                    load_t(b)
                    if b == G - 1:
                        sp.wait_ge(s["acc_ready"], g.at(G, half))
                        sp.dma_start(tailc[:].bitcast(F32), scratch[:, bass.ds(g.index * G + half, half)])\
                            .then_inc(tailc_in, 16)
                    load_n(b)

            body(Phase("a", 0))
            body(Phase("ab", 0))
            with sp.Fori(0, NG - 2) as m:
                body(Phase("abc", m))

        @block.tensor
        def _(pe):
            mm = nc.tensor.matmul

            pe.wait_ge(w_in, W_ALL)
            for i in range(2):
                for j in range(2):
                    last = mm(gb[0][:, i], wxt_raw[:, j, i * P:(i + 1) * P], ww_raw[:, j], start=j == 0,
                              stop=j == 1)
            last.then_inc(s["wz_psum"], 1)
            pe.wait_ge(s["weights_ready"], 1)
            pe.wait_ge(s["tail_split"], 1)

            def body(ph):
                ga, gp, gc = ph.a, ph.b, ph.c
                taken = []

                def tile(name):
                    bank = bank_of(ph, name)
                    taken.append(name)
                    before = filled(ph, name, 0)
                    if not (isinstance(before, int) and before == 0):
                        pe.wait_ge(bank_drained[bank], before)
                    return gb[bank]

                def done(name, last):
                    last.then_inc(bank_filled[bank_of(ph, name)], 1)

                def drained(name):
                    order = order_of(ph.which)
                    ahead = order.index(taken[-1]) - order.index(name) if taken else 0
                    if ahead > 0 and ahead % BANKS == 0:
                        return
                    pe.wait_ge(bank_drained[bank_of(ph, name)], filled(ph, name))

                def turn(name):
                    ln = 0 if name == "XT" else int(name[2]) - 1
                    out_ = tile(name)
                    pe.wait_ge(s["xn_ready"], xn_count(ph, ln))
                    for t in range(2):
                        for c in range(2):
                            last = nc.tensor.transpose(out_[:, c, t * P:(t + 1) * P],
                                                       xn[:, t, c * P:(c + 1) * P], ident)
                    done(name, last)

                def q(p):
                    out_ = tile(f"q{p}")
                    drained("XT")
                    k = 0
                    for c in range(2):
                        for w, x in ((wq_h, xth), (wq_l, xth), (wq_h, xtl)):
                            last = mm(out_[:, 0], w[:, c, p * P:(p + 1) * P], x[:, c], start=k == 0,
                                      stop=k == 5)
                            k += 1
                    done(f"q{p}", last)

                def qk(h):
                    out_ = tile(f"Qk{h}")
                    drained(f"q{h // 2}")
                    for c in range(2):
                        for k, w in enumerate((wk_h, wk_l)):
                            last = mm(out_[:, c], w[:, h, c * P:(c + 1) * P], qs[:, h % 4], start=k == 0,
                                      stop=k == 1)
                    done(f"Qk{h}", last)

                def score(b):
                    pe.wait_ge(s["tlo_ready"], ga.at(G, b + 1))
                    if b == 0:
                        drained("Qk7")
                    if not (ph.which == "a" and b == 0):
                        pe.wait_ge(s["exp_ready"], ga.at(2 * G, 2 * b))
                    if b > 1 or b == 1 and ph.which != "a":
                        pe.wait_ge(s["ptt_ready"], ga.at(2 * G, 2 * b - 2))
                    for r in range(2):
                        o = scores[:, r, 0:LP]
                        r_ = slice(r * P, (r + 1) * P)
                        k = 0
                        for w, x in ((qk_h[:, 0, b, r_], t0h), (qk_l[:, 0, b, r_], t0h),
                                     (qk_h[:, 0, b, r_], t0l), (qk_h[:, 1, b, r_], t1),
                                     (qk_l[:, 1, b, r_], t1)):
                            last = mm(o, w, x[b % 2][:], start=k == 0, stop=k == 4)
                            k += 1
                        if b > 0:
                            last = turn_tail(b - 1, r)
                        last.then_inc(s["scores_ready"], 1)

                def turn_tail(b, r):
                    if r == 0:
                        pe.wait_ge(s["tailp_ready"], ga.at(G, b + 1))
                    return mm(scores[:, r, 384:512], tailp[:, r], ident_r[:], start=True, stop=True)

                def turn_probs(b):
                    pe.wait_ge(s["probs_ready"], ga.at(G, b + 1))
                    if not (ph.which == "a" and b == 0):
                        pe.wait_ge(s["ptl_ready"], ga.at(G, b))
                    for r in range(2):
                        for t in range(LT):
                            last = nc.tensor.transpose(ptp[:, t, r * P:(r + 1) * P],
                                                       probs[:, r, t * P:(t + 1) * P], ident)
                    last.then_inc(s["pt_ready"], 1)

                def pv(b):
                    pe.wait_ge(s["ptl_ready"], ga.at(G, b + 1))
                    pe.wait_ge(s["nlo_ready"], ga.at(G, b + 1))
                    if b % (G // 2) == 0:
                        pe.wait_ge(tailc_in, ga.at(32, 16 * (b // (G // 2) + 1)))
                    if not (ph.which == "a" and b == 0):
                        pe.wait_ge(s["pcl_ready"], ga.at(G, b))
                    n = nat[b % 2]
                    terms = [(n[:, t, lo:lo + P], p_[:, t]) for t in range(LT)
                             for lo, p_ in ((0, pth), (0, ptl), (256, pth))]
                    terms.append((tailc[:, b % (G // 2), 0:P], ptt[:]))
                    for k, (w, x) in enumerate(terms):
                        if k == len(terms) - 1:
                            pe.wait_ge(s["ptt_ready"], ga.at(2 * G, 2 * b + 2))
                        mm(acc[:, 0], w, x, start=k == 0, stop=k == len(terms) - 1)
                    terms = [(n[:, t, P:2 * P], p_[:, t]) for t in range(LT) for p_ in (pth, ptl)]
                    terms.append((tailc[:, b % (G // 2), P:2 * P], ptt[:]))
                    for k, (w, x) in enumerate(terms):
                        last = mm(acc[:, 1], w, x, start=k == 0, stop=k == len(terms) - 1)
                    last.then_inc(s["acc_ready"], 1)

                def wv(p):
                    out_ = tile(f"WV{p}")
                    if p == 0:
                        pe.wait_ge(s["pcl_ready"], gp.at(G, G))
                    terms = [(w[:, c, h], x[:, c, h]) for h in (2 * p, 2 * p + 1) for c in range(2)
                             for w, x in ((wv_h, pc_h), (wv_l, pc_h), (wv_h, pc_l))]
                    for k, (w, x) in enumerate(terms):
                        last = mm(out_[:, 0], w, x, start=k == 0, stop=k == len(terms) - 1)
                    done(f"WV{p}", last)

                def y1():
                    out_ = tile("Y1")
                    drained("WV3")
                    for t in range(2):
                        t_ = slice(t * P, (t + 1) * P)
                        terms = [(o[:, p, t_], w[:, p]) for p in range(4)
                                 for o, w in ((oh, wo_h), (ol, wo_h), (oh, wo_l))]
                        for k, (w, x) in enumerate(terms):
                            last = mm(out_[:, t], w, x, start=k == 0, stop=k == len(terms) - 1)
                    done("Y1", last)

                def project(name):
                    w = {"z": wz, "k": w2[:, 0], "r": w2[:, 2]}[name]
                    out_ = tile(name)
                    drained("XT2")
                    for o in range(2):
                        for c in range(2):
                            last = mm(out_[:, o], w[:, c, o * P:(o + 1) * P], xt[:, c], start=c == 0,
                                      stop=c == 1)
                    done(name, last)

                def v():
                    out_ = tile("v")
                    for t in range(2):
                        for c in range(2):
                            last = mm(out_[:, t], xt[:, c, t * P:(t + 1) * P], w2[:, 1, c], start=c == 0,
                                      stop=c == 1)
                    done("v", last)

                def s_tile(name):
                    j, l0 = int(name[2]), 0 if name[1] == "a" else 2
                    t, rows = j // 2, slice(64 * (j % 2), 64 * (j % 2) + 64)
                    out_ = tile(name)
                    if j == 0:
                        pe.wait_ge(s["hatp_ready"], gp.at(5, l0 + 3))
                        pe.wait_ge(s["hatv_ready"], gp.at(3, l0 + 1))
                    for c in range(2):
                        cols = slice(c * T + t * P, c * T + t * P + P)
                        for l in range(2):
                            last = mm(out_[:, c, l * P:(l + 1) * P], khat[rows, l0 + l, cols],
                                      rhat[rows, l0 + l, cols], start=True, stop=True)
                    done(name, last)

                def o2_():
                    out_ = tile("O2")
                    drained("Sb3")
                    drained("v")
                    for j in range(8):
                        t, h = j // 4, j % 4
                        r0 = 64 * (h % 2)
                        last = mm(out_[r0:r0 + 64, h // 2, t * P:(t + 1) * P],
                                  vt[:, t, h * 64:(h + 1) * 64], s2[:, j], start=True, stop=True)
                    done("O2", last)

                def y2():
                    out_ = tile("Y2")
                    drained("O2")
                    for t in range(2):
                        for c in range(2):
                            last = mm(out_[:, t], o2[:, c, t * P:(t + 1) * P], wo2[:, c], start=c == 0,
                                      stop=c == 1)
                    done("Y2", last)

                def pf_():
                    out_ = tile("Pf")
                    drained("XT3")
                    for c in range(2):
                        last = mm(out_[0:R, 0], u1[:, c], xt3[:, c], start=c == 0, stop=c == 1)
                    done("Pf", last)

                def hidden(i):
                    out_ = tile(f"H{i}")
                    drained("Pf")
                    for c in range(2):
                        f = (2 * i + c) * P
                        last = mm(out_[:, c], v1[:, f:f + P], pf, start=True, stop=True)
                    done(f"H{i}", last)

                def qf_():
                    out_ = tile("Qf")
                    drained("H3")
                    for c in range(8):
                        last = mm(out_[0:R, 0], u2[:, c], hid[:, c], start=c == 0, stop=c == 7)
                    done("Qf", last)

                def y3():
                    out_ = tile("Y3")
                    drained("Qf")
                    for t in range(2):
                        last = mm(out_[:, t], qf[:, t * P:(t + 1) * P], v2, start=True, stop=True)
                    done("Y3", last)

                steps = {"Y1": y1, "v": v, "O2": o2_, "Y2": y2, "Pf": pf_, "Qf": qf_, "Y3": y3}
                for n in ("XT", "XT2", "XT3"):
                    steps[n] = lambda n=n: turn(n)
                for n in "zkr":
                    steps[n] = lambda n=n: project(n)
                for i in range(8):
                    steps[f"Qk{i}"] = lambda i=i: qk(i)
                for i in range(4):
                    for n in (f"Sa{i}", f"Sb{i}"):
                        steps[n] = lambda n=n: s_tile(n)
                    steps[f"q{i}"] = lambda i=i: q(i)
                    steps[f"WV{i}"] = lambda i=i: wv(i)
                    steps[f"H{i}"] = lambda i=i: hidden(i)

                for n in START:
                    if ph.has(n):
                        steps[n]()
                if ga:
                    score(0)
                for n in AFTER_SCORE:
                    if ph.has(n):
                        steps[n]()
                for b in range(G):
                    if ga:
                        turn_probs(b)
                        if b + 1 < G:
                            score(b + 1)
                        else:
                            for r in range(2):
                                last = turn_tail(b, r)
                            last.then_inc(s["tailt_ready"], 1)
                    for n in FILL1[b]:
                        if ph.has(n):
                            steps[n]()
                    if ga:
                        pv(b)
                    for n in FILL2[b]:
                        if ph.has(n):
                            steps[n]()

            turns(pe, body)

        @block.scalar
        def _(act):
            go = nc.scalar.activation

            def body(ph):
                ga, gp, gc = ph.a, ph.b, ph.c

                def wait_tile(name):
                    bank = bank_of(ph, name)
                    act.wait_ge(bank_filled[bank], filled(ph, name))
                    return gb[bank]

                def drain(name, last):
                    last.then_inc(bank_drained[bank_of(ph, name)], 1)

                def t_hi(b):
                    act.wait_ge(ctxt_in[b % 2], ga.at(16 * G // 2, 16 * (b // 2 + 1)))
                    if not (ph.which == "a" and b < 2):
                        act.wait_ge(s["scores_ready"], ga.at(2 * G, 2 * (b - 1)))
                    go(t0h[b % 2][:], raw_t[b % 2][:, 0], ACT.Copy)
                    if not (ph.which == "a" and b < 1):
                        act.wait_ge(s["tlo_ready"], ga.at(G, b))
                    go(t1s[64:128], raw_t[b % 2][64:128, 1], ACT.Copy).then_inc(s["thi_ready"], 1)

                def n_hi(b):
                    act.wait_ge(ctxn_in[b % 2], ga.at(16 * G // 2, 16 * (b // 2 + 1)))
                    if not (ph.which == "a" and b < 2):
                        act.wait_ge(s["acc_ready"], ga.at(G, b - 1))
                    go(nat[b % 2][:, :, 0:C], raw_n[b % 2][:], ACT.Copy).then_inc(s["nhi_ready"], 1)

                def exps(b):
                    for r in range(2):
                        act.wait_ge(s["nmax_ready"], ga.at(2 * G, 2 * b + r + 1))
                        go(probs[:, r, 0:L], scores[:, r, 0:L], ACT.Exp, bias=nmax[:, r:r + 1],
                           accum_out=rsum[:, r:r + 1]).then_inc(s["exp_ready"], 1)

                def pt_hi(b):
                    act.wait_ge(s["pt_ready"], ga.at(G, b + 1))
                    go(pth[:], ptp[:], ACT.Copy).then_inc(s["pth_ready"], 1)

                def pc_hi(b):
                    act.wait_ge(s["acc_ready"], ga.at(G, b + 1))
                    go(pc_h[:, :, :, b * S:(b + 1) * S], acc[:].rearrange("p c (h s) -> p c h s", h=H),
                       ACT.Copy).then_inc(s["pch_ready"], 1)

                def step(n):
                    if n in ("Y1", "Y2", "Y3") or n[0] == "S":
                        return
                    t = wait_tile(n)
                    if n == "XT":
                        go(xth[:], t[:], ACT.Copy).then_inc(s["xthi_ready"], 1)
                    elif n == "XT2":
                        for c in range(2):
                            last = go(xt[:, c], t[:, c], ACT.Identity, scale=vecs[:, c:c + 1],
                                      bias=vecs[:, 2 + c:3 + c])
                        drain(n, last)
                    elif n == "XT3":
                        drain(n, go(xt3[:], t[:], ACT.Copy))
                    elif n[0] == "q":
                        p = int(n[1])
                        for i in range(2):
                            last = go(qs[0:64, (2 * p + i) % 4], t[64 * i:64 * i + 64, 0], ACT.Copy)
                        last.then_inc(s["qhi_ready"], 1)
                    elif n[:2] == "Qk":
                        h = int(n[2])
                        go(qk_h[:, :, :, h * S:(h + 1) * S],
                           t[:].rearrange("p c (b s) -> p c b s", b=G), ACT.Copy)\
                            .then_inc(s["qkhi_ready"], 1)
                    elif n[:2] == "WV":
                        go(oh[:, int(n[2])], t[:, 0], ACT.Copy).then_inc(s["oh_ready"], 1)
                    elif n == "z":
                        for c in range(2):
                            last = go(at[:, c], t[:, c], ACT.Tanh, scale=0.5, bias=vecs[:, 4 + c:5 + c])
                        last.then_inc(s["tanh_ready"], 1)
                        act.wait_ge(s["tanh_ready"], gp.at(2, 1))
                        drain(n, go(at[:], at[:], ACT.Copy, scale=-0.5, bias=0.5))
                    elif n == "r":
                        go(rt_[:], t[:], ACT.Tanh, scale=0.5).then_inc(s["tanh_ready"], 1)
                        act.wait_ge(s["tanh_ready"], gp.at(2, 2))
                        drain(n, go(rt_[:], rt_[:], ACT.Copy, scale=0.5, bias=0.5))
                    elif n == "k":
                        drain(n, go(kt[:], t[:], ACT.Copy))
                    elif n == "v":
                        if gc:
                            act.wait_ge(out_done, gc.at(16, 16))
                        drain(n, go(vt[:], t[:], ACT.Copy))
                    elif n == "O2":
                        drain(n, go(o2, t[:], ACT.Copy))
                    elif n == "Pf":
                        drain(n, go(pf, t[0:R, 0], ACT.Copy))
                    elif n[0] == "H":
                        i = int(n[1])
                        for c in range(2):
                            f = 2 * i + c
                            last = go(hid[:, f], t[:, c], ACT.Gelu_apprx_tanh, bias=vecs[:, 6 + f:7 + f])
                        drain(n, last)
                    elif n == "Qf":
                        drain(n, go(qf, t[0:R, 0], ACT.Copy))

                if ga:
                    t_hi(0)
                for n in START:
                    if ph.has(n):
                        step(n)
                    if n == "q1" and ga:
                        t_hi(1)
                        n_hi(0)
                if ga:
                    exps(0)
                for n in AFTER_SCORE:
                    if ph.has(n):
                        step(n)
                for b in range(G):
                    if ga:
                        if b + 2 < G:
                            t_hi(b + 2)
                        pt_hi(b)
                        if b + 1 < G:
                            exps(b + 1)
                    for n in FILL1[b]:
                        if ph.has(n):
                            step(n)
                    if ga:
                        if b + 1 < G:
                            n_hi(b + 1)
                        pc_hi(b)
                    for n in FILL2[b]:
                        if ph.has(n):
                            step(n)
                    if gc and b == 1:
                        act.wait_ge(bank_drained[bank_of(ph, "Y3")], filled(ph, "Y3"))
                        act.dma_start(out_v[gc.index], ob[:]).then_inc(out_done, 16)

            act.wait_ge(s["weights_ready"], 1)
            turns(act, body)
            act.wait_ge(out_done, 16 * NG)

        @block.vector
        def _(dve):
            v_ = nc.vector
            chain = Chain(dve, s["dve_chain"], DVE_SETUP, DVE_LINKS)
            link, sign, need = chain.link, chain.sign, chain.need

            for buf in (tailp[:].bitcast(F32), s2[:], tail3[:].bitcast(F32)):
                v_.memset(buf, 0.0)
            v_.memset(vecs[:, 14:16], -0.5)
            v_.memset(eps2[:], EPS)
            v_.memset(probs[:], 0.0)
            v_.memset(t1s[0:64].bitcast(F32), 0.0)
            link(v_.memset(fw[:], 1.0))
            dve.wait_ge(w_in, W_ALL)
            link(v_.tensor_copy(tail3[:, 0, 0:C], tail_raw[:]))
            v_.tensor_copy(tail3[:, 2, 0:C], tail_raw[:])
            v_.tensor_tensor(tail3[:, 1, 0:P], tail_raw[:, 0:P], tail3[:, 0, 0:P].bitcast(F32), ALU.subtract)
            for i in (0, 2):
                last = v_.tensor_tensor(tail3[:, i, C:256], tail_raw[:, P:C], tail3[:, 0, P:C].bitcast(F32),
                                        ALU.subtract)
            last.then_inc(s["tail_split"], 1)
            v_.tensor_copy(ident_r[:], ident_raw[:])
            v_.tensor_copy(mask[:], mask_raw[:])
            v_.tensor_scalar(vecs[:, 4:6], bw_raw[:], 0.5, None, ALU.mult)
            v_.tensor_copy(wq_h[:], wq_raw[:])
            v_.tensor_copy(wo_h[:], wo_raw[:])
            v_.tensor_copy(wv_h[:], wv_raw[:])
            link(v_.tensor_scalar(wk_h[:], wk_raw[:], SCALE, None, ALU.mult))
            v_.tensor_tensor(wq_l[:], wq_raw[:], wq_h[:].bitcast(F32), ALU.subtract)
            v_.tensor_tensor(wo_l[:], wo_raw[:], wo_h[:].bitcast(F32), ALU.subtract)
            v_.tensor_tensor(wv_l[:], wv_raw[:], wv_h[:].bitcast(F32), ALU.subtract)
            v_.scalar_tensor_tensor(wk_l[:], wk_raw[:], SCALE, wk_h[:].bitcast(F32), ALU.mult, ALU.subtract)
            dve.wait_ge(s["wz_psum"], 1)
            v_.tensor_copy(wz[:], gb[0][:]).then_inc(s["weights_ready"], 1)
            assert chain.k == DVE_SETUP, chain.k

            def body(ph):
                ga, gp, gc = ph.a, ph.b, ph.c
                chain.begin(ph)
                held, marks = [], {}

                def wait_tile(name):
                    bank = bank_of(ph, name)
                    dve.wait_ge(bank_filled[bank], filled(ph, name))
                    return gb[bank]

                def drain(name, last):
                    last.then_inc(bank_drained[bank_of(ph, name)], 1)

                def own_drain(name):
                    dve.wait_ge(bank_drained[bank_of(ph, name)], filled(ph, name))

                def hold(k=0):
                    if held or k:
                        need(max([k] + held))
                    held.append(sign(v_.memset(cell[:], 0.0)))

                def norm_stats(x, ln):
                    v_.bn_stats(stats[:, 0], x[:, 0])
                    hold(sign(v_.bn_stats(stats[:, 1], x[:, 1])))
                    for t in range(2):
                        last = v_.bn_aggr(mv[:, ln, t], stats[:, t])
                    link(last)
                    v_.tensor_scalar(ve[:, ln], mv[:, ln, :, 1], EPS, None, ALU.add)\
                        .then_inc(s["var_ready"], 1)

                def norm_apply(x, ln):
                    dve.wait_ge(s["rstd_ready"], vars_before(ph) if ln == 2 else var_count(ph, ln))
                    k = 3 if ln == 1 else ln
                    for t in range(2):
                        last = v_.tensor_scalar(xn[:, t], x[:, t], mv[:, ln, t, 0:1], rstd[:, k, t:t + 1],
                                                ALU.subtract, ALU.mult)
                    last.then_inc(s["xn_ready"], 1)

                def nmaxs(b):
                    for r in range(2):
                        dve.wait_ge(s["scores_ready"], ga.at(2 * G, 2 * b + r + 1))
                        if b > 0:
                            tail_out(b - 1, r)
                        v_.tensor_reduce(nmax[:, r:r + 1], scores[:, r, 0:L], AX.X, ALU.max, negate=True)\
                            .then_inc(s["nmax_ready"], 1)

                def tail_out(b, r):
                    v_.tensor_copy(ptt[:, r * P:(r + 1) * P], scores[0:3, r, 384:512]).then_inc(s["ptt_ready"], 1)

                def norm_probs(b):
                    dve.wait_ge(s["exp_ready"], ga.at(2 * G, 2 * b + 2))
                    link(v_.reciprocal(rinv[:], rsum[:]))
                    for r in range(2):
                        last = v_.tensor_scalar(probs[:, r, 0:L], probs[:, r, 0:L], rinv[:, r:r + 1], None,
                                                ALU.mult)
                    last.then_inc(s["probs_ready"], 1)

                def tail_parts(b):
                    dve.wait_ge(s["probs_ready"], ga.at(G, b + 1))
                    for i in range(2):
                        last = v_.tensor_copy(tailp[:, :, i:i + 1], probs[:, :, L - 1:L])
                    link(last)
                    v_.tensor_tensor(tailp[:, :, 2:3], probs[:, :, L - 1:L], tailp[:, :, 0:1].bitcast(F32),
                                     ALU.subtract).then_inc(s["tailp_ready"], 1)

                def pt_lo(b):
                    dve.wait_ge(s["pth_ready"], ga.at(G, b + 1))
                    v_.tensor_tensor(ptl[:], ptp[:], pth[:].bitcast(F32), ALU.subtract)\
                        .then_inc(s["ptl_ready"], 1)

                def pc_lo(b):
                    dve.wait_ge(s["pch_ready"], ga.at(G, b + 1))
                    b_ = slice(b * S, (b + 1) * S)
                    v_.tensor_tensor(pc_l[:, :, :, b_], acc[:].rearrange("p c (h s) -> p c h s", h=H),
                                     pc_h[:, :, :, b_].bitcast(F32), ALU.subtract)\
                        .then_inc(s["pcl_ready"], 1)

                def decay_step(n):
                    a_flat = at[:].rearrange("p c t -> p (c t)")
                    k_flat = kt[:].rearrange("p c t -> p (c t)")
                    a4, f4, b4, p4 = (x.rearrange("p (n i) -> p n i", i=4)
                                      for x in (a_flat, fw[:], bw_[:], pw[:]))

                    def two(x, l):
                        return x.rearrange("p (m h i) -> p m h i", h=2, i=2 << l)

                    i = int(n[1]) if n[-1].isdigit() else 0
                    if n == "f1":
                        dve.wait_ge(bank_drained[bank_of(ph, "z")], filled(ph, "z"))
                        marks[n] = sign(v_.tensor_scalar(f4[:, :, 1:2], a4[:, :, 1:2], A_MIN, None, ALU.max))
                    elif n[0] == "f":
                        need(marks[f"f{i - 1}"])
                        out_ = v_.scalar_tensor_tensor(f4[:, :, i:i + 1], a4[:, :, i:i + 1], A_MIN,
                                                       f4[:, :, i - 1:i], ALU.max, ALU.mult)
                        if i == 3:
                            out_.then_inc(s["f_ready"], 1)
                        else:
                            marks[n] = sign(out_)
                    elif n[0] == "i":
                        if i == 1:
                            v_.memset(b4[:, :, 0:1], 1.0)
                        if i == 3:
                            dve.wait_ge(s["f_ready"], gp.at(1, 1))
                        else:
                            need(marks[f"f{i}"])
                        out_ = v_.reciprocal(b4[:, :, i:i + 1], f4[:, :, i:i + 1])
                        if i == 3:
                            out_.then_inc(s["inv_ready"], 1)
                    elif n == "pw":
                        dve.wait_ge(s["f_ready"], gp.at(1, 1))
                        v_.scalar_tensor_tensor(p4, a4[:, :, 0:1].to_broadcast([P, T // 2, 4]), A_MIN, f4,
                                                ALU.max, ALU.mult).then_inc(s["pw_ready"], 1)
                    elif n == "bw":
                        dve.wait_ge(s["inv_ready"], gp.at(1, 1))
                        dve.wait_ge(s["pw_ready"], gp.at(LEVELS - 1, 1))
                        marks[n] = sign(v_.tensor_tensor(a4, b4, f4[:, :, 3:4].to_broadcast([P, T // 2, 4]),
                                                         ALU.mult))
                    elif n[0] == "k":
                        if i == 1:
                            dve.wait_ge(bank_drained[bank_of(ph, "k")], filled(ph, "k"))
                        if i == 3:
                            wait_tile("v")
                        need(marks[("bw", "b1", "b2")[i - 1]])
                        v_.tensor_tensor(khat[:, i], k_flat, a_flat, ALU.mult).then_inc(s["hatv_ready"], 1)
                    elif n[0] == "b":
                        dve.wait_ge(s["hatv_ready"], gp.at(3, i))
                        b_, p_ = two(a_flat, i), two(pw[:], i)
                        marks[n] = sign(v_.tensor_tensor(
                            b_[:, :, 0], b_[:, :, 0],
                            p_[:, :, 1, (2 << i) - 1:2 << i].to_broadcast([P, 2 * T // (4 << i), 2 << i]),
                            ALU.mult))
                    else:
                        dve.wait_ge(s["hatp_ready"], gp.at(5, i + 2))
                        need(marks[f"b{i}"])
                        p_ = two(pw[:], i)
                        v_.tensor_tensor(p_[:, :, 1], p_[:, :, 1],
                                         p_[:, :, 0, (2 << i) - 1:2 << i].to_broadcast(
                                             [P, 2 * T // (4 << i), 2 << i]),
                                         ALU.mult).then_inc(s["pw_ready"], 1)

                def step(n):
                    if n == "XT":
                        t = wait_tile(n)
                        dve.wait_ge(s["xthi_ready"], ga.at(1, 1))
                        drain(n, v_.tensor_tensor(xtl[:], t[:], xth[:].bitcast(F32), ALU.subtract))
                    elif n[0] == "q":
                        p = int(n[1])
                        t = wait_tile(n)
                        dve.wait_ge(s["qhi_ready"], ga.at(4, p + 1))
                        for i in range(2):
                            h = (2 * p + i) % 4
                            last = v_.tensor_tensor(qs[64:128, h], t[64 * i:64 * i + 64, 0],
                                                    qs[0:64, h].bitcast(F32), ALU.subtract)
                        drain(n, last)
                    elif n[:2] == "Qk":
                        h = int(n[2])
                        t = wait_tile(n)
                        dve.wait_ge(s["qkhi_ready"], ga.at(H, h + 1))
                        h_ = slice(h * S, (h + 1) * S)
                        drain(n, v_.tensor_tensor(qk_l[:, :, :, h_], t[:].rearrange("p c (b s) -> p c b s", b=G),
                                                  qk_h[:, :, :, h_].bitcast(F32), ALU.subtract))
                    elif n[:2] == "WV":
                        p = int(n[2])
                        t = wait_tile(n)
                        dve.wait_ge(s["oh_ready"], gp.at(4, p + 1))
                        drain(n, v_.tensor_tensor(ol[:, p], t[:, 0], oh[:, p].bitcast(F32), ALU.subtract))
                    elif n == "Y1":
                        dve.wait_ge(s["xb_ready"], gp.at(1, 1))
                        if gc:
                            dve.wait_ge(s["ob_ready"], gp.at(1, 0))
                        drain(n, v_.tensor_tensor(x12[:], wait_tile(n)[:], xb[:], ALU.add))
                        own_drain(n)
                        norm_stats(x12, 1)
                    elif n[0] == "S":
                        j, l0 = int(n[2]), 0 if n[1] == "a" else 2
                        t = wait_tile(n)
                        if l0:
                            own_drain(f"Sa{j}")
                        first = 4 * (j // 2) + j % 2
                        k = 0
                        for l in range(2):
                            hold(k)
                            i = v_.copy_predicated(
                                s2[:, first:first + 3:2],
                                mask[:, l0 + l:l0 + l + 1].to_broadcast([P, 2, P]), t[:, :, l * P:(l + 1) * P])
                            if l == 0:
                                k = sign(i)
                        drain(n, i)
                    elif n == "Y2":
                        drain(n, v_.tensor_tensor(x12[:], wait_tile(n)[:], x12[:], ALU.add))
                        own_drain(n)
                        norm_stats(x12, 2)
                    elif n == "Y3":
                        t = wait_tile(n)
                        dve.wait_ge(s["ob_ready"], gc.at(1, 1))
                        drain(n, v_.tensor_tensor(ob[:], t[:], ob[:], ALU.add))
                    elif n in GAP_STEPS:
                        decay_step(n)

                def gap(b, i):
                    for n in GAPS[b][i]:
                        if gc if n == "Y3" else gp:
                            step(n)

                if ga:
                    dve.wait_ge(x_in, ga.at(16, 16))
                    norm_stats(xin, 0)
                for n in START:
                    if n == "WV1" and gc:
                        norm_apply(x12, 2)
                    if n == "WV2" and ga:
                        if gc:
                            wait_tile("XT3")
                        norm_apply(xin, 0)
                    if n == "Qk7" and gp:
                        norm_apply(x12, 1)
                    if ph.has(n):
                        step(n)
                if ga:
                    nmaxs(0)
                    norm_probs(0)
                    tail_parts(0)
                for b in range(G):
                    gap(b, 0)
                    if ga:
                        pt_lo(b)
                        if b + 1 < G:
                            nmaxs(b + 1)
                        else:
                            dve.wait_ge(s["tailt_ready"], ga.at(1, 1))
                            for r in range(2):
                                tail_out(b, r)
                    gap(b, 1)
                    if ga and b + 1 < G:
                        norm_probs(b + 1)
                        tail_parts(b + 1)
                    gap(b, 2)
                    if ga:
                        pc_lo(b)
                    gap(b, 3)
                if ph.which != "c":
                    assert chain.k == DVE_LINKS[ph.which], chain.k

            turns(dve, body)

        @block.gpsimd
        def _(pool):
            p_ = nc.gpsimd
            chain = Chain(pool, s["pool_chain"], 0, POOL_LINKS)

            def body(ph):
                ga, gp, gc = ph.a, ph.b, ph.c
                chain.begin(ph)
                link = chain.link
                half = vecs[:, 14:16]

                def t_lo(b):
                    pool.wait_ge(s["thi_ready"], ga.at(G, b + 1))
                    i = b % 2
                    p_.tensor_tensor(t0l[i][:], raw_t[i][:, 0], t0h[i][:].bitcast(F32), ALU.subtract)
                    p_.tensor_tensor(t1[i][:], raw_t[i][:, 1], t1s[:].bitcast(F32), ALU.subtract)\
                        .then_inc(s["tlo_ready"], 1)

                def n_lo(b):
                    pool.wait_ge(s["nhi_ready"], ga.at(G, b + 1))
                    i = b % 2
                    p_.tensor_tensor(nat[i][:, :, 256:384], raw_n[i][:, :, 0:P],
                                     nat[i][:, :, 0:P].bitcast(F32), ALU.subtract)
                    p_.tensor_tensor(nat[i][:, :, C:256], raw_n[i][:, :, P:C],
                                     nat[i][:, :, P:C].bitcast(F32), ALU.subtract)\
                        .then_inc(s["nlo_ready"], 1)

                def rstds(ln):
                    pool.wait_ge(s["var_ready"], var_count(ph, ln))
                    i = p_.tensor_tensor(rstd[:, ln], ve[:, ln], half, ALU.pow)
                    if ln == 1:
                        link(i)
                        link(p_.tensor_tensor(rstd[:, 3], mv[:, 1, :, 1], rstd[:, 1], ALU.mult))
                        link(p_.tensor_tensor(rstd[:, 3], rstd[:, 3], rstd[:, 1], ALU.mult))
                        link(p_.tensor_tensor(rstd[:, 3], rstd[:, 3], eps2[:], ALU.add))
                        link(p_.tensor_tensor(rstd[:, 3], rstd[:, 3], half, ALU.pow))
                        i = p_.tensor_tensor(rstd[:, 3], rstd[:, 3], rstd[:, 1], ALU.mult)
                    i.then_inc(s["rstd_ready"], 1)

                def hats(l):
                    r_flat = rt_[:].rearrange("p c t -> p (c t)")
                    if l == 0:
                        pool.wait_ge(bank_drained[bank_of(ph, "r")], filled(ph, "r"))
                        pool.wait_ge(s["f_ready"], gp.at(1, 1))
                        p_.tensor_tensor(rhat[:, 0], r_flat, fw[:], ALU.mult).then_inc(s["hatp_ready"], 1)
                        pool.wait_ge(bank_drained[bank_of(ph, "k")], filled(ph, "k"))
                        pool.wait_ge(s["inv_ready"], gp.at(1, 1))
                        p_.tensor_tensor(khat[:, 0], kt[:].rearrange("p c t -> p (c t)"), bw_[:], ALU.mult)\
                            .then_inc(s["hatp_ready"], 1)
                    else:
                        pool.wait_ge(s["pw_ready"], gp.at(LEVELS - 1, l))
                        p_.tensor_tensor(rhat[:, l], r_flat, pw[:], ALU.mult).then_inc(s["hatp_ready"], 1)

                if ga:
                    t_lo(0)
                    rstds(0)
                    t_lo(1)
                    n_lo(0)
                if gp:
                    rstds(1)
                if ga:
                    pool.wait_ge(s["xn_ready"], xn_count(ph, 0))
                    p_.tensor_tensor(xb[:], xin[:], bo[:].rearrange("p (o d) -> p o d", o=1).to_broadcast([P, 2, D]),
                                     ALU.add).then_inc(s["xb_ready"], 1)
                for b in range(G):
                    if gp:
                        for l in {2: [0, 1], 3: [2], 4: [3]}.get(b, []):
                            hats(l)
                    if ga:
                        if b + 2 < G:
                            t_lo(b + 2)
                        if b + 1 < G:
                            n_lo(b + 1)
                    if gp and b == 7:
                        rstds(2)
                        p_.tensor_tensor(ob[:], x12[:], b2[:].rearrange("p (o d) -> p o d", o=1).to_broadcast([P, 2, D]),
                                         ALU.add).then_inc(s["ob_ready"], 1)
                if ph.which != "c":
                    assert chain.k == POOL_LINKS[ph.which], chain.k

            pool.wait_ge(s["weights_ready"], 1)
            turns(pool, body)


def var_count(phase, ln):
    return vars_before(phase) + (ln + 1 if phase.a else ln)


def vars_before(phase):
    return phase.before({"a": 1, "ab": 3, "abc": 3, "bc": 2}.get)


def xn_count(phase, ln):
    here = [l for l, group in ((2, phase.c), (0, phase.a), (1, phase.b)) if group]
    return phase.before({"a": 1, "ab": 2, "abc": 3, "bc": 2}.get) + here.index(ln) + 1


def level_masks():
    t = np.arange(P)
    key, query = t[:, None], t[None, :]
    masks = [(key // 4 == query // 4) & (key <= query)]
    for n in (4, 8, 16):
        masks.append((key // (2 * n) == query // (2 * n)) & (key // n < query // n))
    return np.stack(masks, 1).astype(np.float32)


def chunks(w, p=P):
    return np.ascontiguousarray(w.reshape(-1, p, w.shape[-1]).transpose(1, 0, 2))


def kernel(x, ctx_768, L0_xattn_Wq, L0_xattn_Wk, L0_xattn_Wv, L0_xattn_Wo, L0_xattn_bo, L0_attn_ln_g,
           L0_attn_ln_b, L0_attn_Wx, L0_attn_Ww, L0_attn_bw, L0_attn_Wk, L0_attn_Wv, L0_attn_Wr,
           L0_attn_Wo, L0_ffn_U1, L0_ffn_V1, L0_ffn_b1, L0_ffn_U2, L0_ffn_V2, L0_ffn_b2):
    import concourse.bacc as bacc
    from concourse.bass_utils import run_bass_kernel_spmd

    c = np.asarray(ctx_768)
    ctx_t = np.zeros((B, P, 2, LP), c.dtype)
    ct = c.transpose(0, 2, 1)
    ctx_t[:, :, 0, :L] = ct[:, :P]
    ctx_t[:, :64, 1, :L] = ct[:, P:]
    ctx_t[:, 64:, 1, :L] = ct[:, P:]
    ctx_n = np.ascontiguousarray(c[:, :LT * P].reshape(B, LT, P, C).transpose(0, 2, 1, 3))
    wk = np.asarray(L0_xattn_Wk).T.reshape(H, DH, C).transpose(1, 0, 2)
    wk = np.concatenate([wk, wk[:, :, P:]], 2)
    wk = np.concatenate([wk, wk], 0)
    wv_ = np.asarray(L0_xattn_Wv)
    wv = np.zeros((P, 2, H, P), wv_.dtype)
    for h in range(H):
        o = 64 * (h % 2)
        wv[:, 0, h, o:o + 64] = wv_[:P, h * 64:(h + 1) * 64]
        wv[:64, 1, h, o:o + 64] = wv_[P:, h * 64:(h + 1) * 64]
        wv[64:, 1, h, o:o + 64] = wv_[P:, h * 64:(h + 1) * 64]

    def column(v):
        return np.ascontiguousarray(np.asarray(v).reshape(-1, P).T)

    def rows(v):
        return np.ascontiguousarray(np.broadcast_to(np.asarray(v), (P, D)))

    arrays = {
        "x": np.ascontiguousarray(np.asarray(x).reshape(B * S, D)), "ctx_t": ctx_t, "ctx_n": ctx_n,
        "ctx_tail": np.ascontiguousarray(c[:, L - 1]),
        "wq": chunks(np.asarray(L0_xattn_Wq)), "wk": wk, "wv": wv, "wo": chunks(np.asarray(L0_xattn_Wo)),
        "bo": rows(L0_xattn_bo), "ln_g": column(L0_attn_ln_g), "ln_b": column(L0_attn_ln_b),
        "wxt": chunks(np.asarray(L0_attn_Wx).T), "ww": chunks(np.asarray(L0_attn_Ww)),
        "bw": column(L0_attn_bw), "wk2": chunks(np.asarray(L0_attn_Wk)),
        "wv2": chunks(np.asarray(L0_attn_Wv)), "wr2": chunks(np.asarray(L0_attn_Wr)),
        "wo2": chunks(np.asarray(L0_attn_Wo)), "u1": chunks(np.asarray(L0_ffn_U1)),
        "v1": np.asarray(L0_ffn_V1), "b1": column(L0_ffn_b1), "u2": chunks(np.asarray(L0_ffn_U2)),
        "v2": np.asarray(L0_ffn_V2), "b2": rows(L0_ffn_b2),
        "ident": np.eye(P, dtype=np.float32), "mask": level_masks(),
    }
    nc = bacc.Bacc("TRN2", target_bir_lowering=False, num_devices=1)
    a = {n: nc.dram_tensor(f"in_{n}", v.shape, mybir.dt.from_np(v.dtype), kind="ExternalInput").ap()
         for n, v in arrays.items()}
    out = nc.dram_tensor("out", (B * S, D), F32, kind="ExternalOutput").ap()
    build(nc, a, out)
    r = run_bass_kernel_spmd(nc, [{f"in_{n}": v for n, v in arrays.items()}], core_ids=[0])
    return r.results[0]["out"].reshape(B, S, D)
```

```python
from contextlib import ExitStack

import concourse.bass as bass
import concourse.mybir as mybir
import numpy as np

F32 = mybir.dt.float32
F32R = mybir.dt.float32r
U8 = mybir.dt.uint8
ACT = mybir.ActivationFunctionType
ALU = mybir.AluOpType
AX = mybir.AxisListType

B, S, D = 128, 32, 256
L, C = 257, 192
H, DH = 8, 64
INNER = H * DH
F, R = 1024, 64
G = 8
NG = B // G
T = G * S
P = 128
LP = L + 1
LT = 2
SCALE = DH ** -0.5
EPS = 1e-5
A_MIN = 2.0 ** -25
LEVELS = 4

START = ["WV0", "WV1", "XT", "XT3", "Pf", "q0", "H0", "q1", "Y1", "Qk0", "H1", "Qk1", "q2", "Qk2", "H2", "Qk3",
         "q3", "H3", "Qk4", "XT2", "Qk5", "Qk6", "Qk7", "z"]
AFTER_SCORE = ["Qf"]
FILL1 = [["k"], ["r"], ["v"], ["Sa0", "Sa1"], ["Sa2", "Sa3"], ["Sb0", "Sb1"], ["Sb3"], ["O2"]]
FILL2 = [["Y3"], [], [], [], [], ["Sb2"], [], ["Y2"]]
GAPS = [[["f1", "i1", "f2"], ["i2"], [], ["f3"]],
        [["i3"], ["Y3"], ["pw"], []],
        [["bw"], ["k1"], ["b1"], ["p1"]],
        [[], ["Sa0"], ["b2"], ["p2"]],
        [["Sa1"], ["Sa2"], ["Sa3"], []],
        [[], ["Sb0"], ["Sb1"], []],
        [["Sb2"], ["Sb3"], [], []],
        [[], [], [], []]]
POOL_HATS = [([], [])] * 2 + [(["r0", "r1"], ["k0"]), (["r2", "k2"], []), (["r3", "k3"], [])] + [([], [])] * 3
HAT_ORDER = [n for before, behind in POOL_HATS for n in before + behind]
HATS = len(HAT_ORDER)
GAP_STEPS = {n for gaps in GAPS for gap in gaps for n in gap if n[0] in "fipbk"}
A_STEPS = {"XT"} | {f"q{p}" for p in range(4)} | {f"Qk{h}" for h in range(H)}
C_STEPS = {f"H{i}" for i in range(4)} | {"XT3", "Pf", "Qf", "Y3"}
BANK_ORDER = START + AFTER_SCORE + [n for b in range(G) for n in FILL1[b] + FILL2[b]]
BANKS = 4


class Group:

    def __init__(self, register, plus):
        self.register, self.plus = register, plus
        self.index = register + plus

    def at(self, per_group, k):
        return self.register * per_group + (self.plus * per_group + k)


class Phase:

    def __init__(self, which, m):
        self.which, self.m = which, m
        self.a, self.b, self.c = {
            "a": (Group(0, 0), None, None), "ab": (Group(0, 1), Group(0, 0), None),
            "abc": (Group(m, 2), Group(m, 1), Group(m, 0)),
            "bc": (None, Group(0, NG - 1), Group(0, NG - 2)), "c": (None, None, Group(0, NG - 1))}[which]

    def group_of(self, name):
        return self.a if name in A_STEPS else self.c if name in C_STEPS else self.b

    def has(self, name):
        return self.group_of(name) is not None

    def before(self, count):
        total = 0
        for which in ("a", "ab", "abc", "bc"):
            if which == self.which:
                return total if which != "abc" else self.m * count(which) + total
            total += count(which) * (NG - 2 if which == "abc" else 1)
        return total


def order_of(which):
    phase = Phase(which, 0)
    return [n for n in BANK_ORDER if phase.has(n)]


def bank_of(phase, name):
    return order_of(phase.which).index(name) % BANKS


def filled(phase, name, k=1):
    bank = bank_of(phase, name)
    here = order_of(phase.which).index(name) // BANKS + k
    return phase.before(lambda which: len(order_of(which)[bank::BANKS])) + here


def y2_before(phase):
    size = {which: len(order_of(which)) for which in ("ab", "abc", "bc")}
    assert size["ab"] % BANKS == size["abc"] % BANKS
    bank = (size["bc" if phase.which == "c" else "abc"] - 1) % BANKS
    return bank, phase.before(lambda which: len(order_of(which)[bank::BANKS]))


class Chain:

    def __init__(self, engine, sem, setup, counts):
        self.engine, self.sem, self.setup, self.counts = engine, sem, setup, counts
        self.k, self.base = 0, 0

    def begin(self, phase):
        self.k = 0
        self.base = phase.before(lambda which: self.counts[which]) + self.setup

    def sign(self, instruction):
        instruction.then_inc(self.sem, 1)
        self.k += 1
        return self.k

    def need(self, k):
        self.engine.wait_ge(self.sem, self.base + k)

    def link(self, instruction):
        self.need(self.sign(instruction))


DVE_SETUP = 3
DVE_LINKS = {"a": 19, "ab": 51, "abc": 54, "bc": 35, "c": 3}
POOL_LINKS = {"a": 0, "ab": 5, "abc": 5, "bc": 5}


def build(nc, a, out):
    with ExitStack() as ctx:
        def sb(name, shape, dt=F32):
            return ctx.enter_context(nc.sbuf_tensor(name, shape, dt))

        def ps(name, shape):
            return ctx.enter_context(nc.psum_tensor(name, shape, F32))

        def sem(name):
            return ctx.enter_context(nc.semaphore(name))

        wq_h, wq_l = sb("wq_h", [P, 2, INNER], F32R), sb("wq_l", [P, 2, INNER], F32R)
        wk_h, wk_l = sb("wk_h", [P, H, 256], F32R), sb("wk_l", [P, H, 256], F32R)
        wv_h, wv_l = sb("wv_h", [P, 2, H, P], F32R), sb("wv_l", [P, 2, H, P], F32R)
        wo_h, wo_l = sb("wo_h", [P, 4, D], F32R), sb("wo_l", [P, 4, D], F32R)
        w2 = sb("w2", [P, 3, 2, D])
        wz = sb("wz", [P, 2, D])
        wo2 = sb("wo2", [P, 2, D])
        u1, u2 = sb("u1", [P, 2, R]), sb("u2", [P, 8, R])
        v12 = sb("v12", [P, F])
        v1, v2 = v12[0:R], v12[R:2 * R, 0:D]
        bo, b2 = sb("bo", [P, D]), sb("b2", [P, D])
        vecs = sb("vecs", [P, 16])
        ident_r = sb("ident_r", [P, P], F32R)
        ident = ident_r[:].bitcast(F32)
        mask = sb("mask", [P, LEVELS, P], U8)

        raw_t = [sb(f"raw_t{i}", [P, 2, LP]) for i in range(2)]
        raw_n = [sb(f"raw_n{i}", [P, LT, C]) for i in range(2)]
        t0h = [sb(f"t0h{i}", [P, LP], F32R) for i in range(2)]
        t0l = [sb(f"t0l{i}", [P, LP], F32R) for i in range(2)]
        t1 = [sb(f"t1_{i}", [P, LP], F32R) for i in range(2)]
        t1s = sb("t1s", [P, LP], F32R)
        nat = [sb(f"nat{i}", [P, LT, 384], F32R) for i in range(2)]
        probs = sb("probs", [P, 2, LP])
        tailp = sb("tailp", [P, 2, P], F32R)
        pth, ptl = sb("pth", [P, LT, 256], F32R), sb("ptl", [P, LT, 256], F32R)
        ptt = sb("ptt", [3, 256], F32R)
        nmax, rsum, rinv = sb("nmax", [P, 2]), sb("rsum", [P, 2]), sb("rinv", [P, 2])

        cell, eps2 = sb("cell", [1, 1]), sb("eps2", [P, 2])

        tailc = sb("tailc", [3, 4, 256], F32R)
        xin, xb, x12 = (sb(n, [P, 2, D]) for n in ("xin", "xb", "x12"))
        xn = sb("xn", [P, 2, D])
        stats, mv = sb("stats", [P, 2, 6]), sb("mv", [P, 3, 2, 2])
        ve, rstd = sb("ve", [P, 3, 2]), sb("rstd", [P, 4, 2])
        at, vt = sb("at", [P, 2, T]), sb("vt", [P, 2, T])
        fw = sb("fw", [P, 2 * T])
        ob = vt
        s2 = sb("s2", [P, 8, P])
        pq = sb("pq", [P, T])
        pf, qf = pq[0:R], pq[R:2 * R]

        KB = 1024
        base = (nc.sbuf_usable_end - 88 * KB) // 32 * 32
        assert nc.sbuf_base <= base, (nc.sbuf_base, base)

        def at_(name, shape, dt, offset):
            return nc.alloc_sbuf_tensor_at(name, shape, dt, offset=base + offset)

        hid = at_("hid", [P, 8, T], F32, 0)
        oh = at_("oh", [P, 4, T], F32R, 8 * KB)
        ol = at_("ol", [P, 4, T], F32R, 12 * KB)
        rhat = at_("rhat", [P, LEVELS, 2 * T], F32, 0)
        khat = at_("khat", [P, LEVELS, 2 * T], F32, 8 * KB)
        xt = at_("xt", [P, 2, T], F32, 14 * KB)
        xt3 = at_("xt3", [P, 2, T], F32, 6 * KB)
        xn3 = at_("xn3", [P, 2, D], F32, 0)
        xth = at_("xth", [P, 2, T], F32R, 80 * KB)
        xtl = at_("xtl", [P, 2, T], F32R, 82 * KB)
        qs = at_("qs", [P, 4, T], F32R, 84 * KB)
        kt = at_("kt", [P, 2, T], F32, 80 * KB)
        rt_ = at_("rt", [P, 2, T], F32, 82 * KB)
        bw_ = at_("bwd", [P, 2 * T], F32, 84 * KB)
        pw = at_("pw", [P, 2 * T], F32, 86 * KB)
        o2 = pw[:].rearrange("p (c t) -> p c t", c=2)

        qk_h = at_("qk_h", [P, 2, G, 256], F32R, 16 * KB)
        qk_l = at_("qk_l", [P, 2, G, 256], F32R, 32 * KB)
        pc_h = at_("pc_h", [P, 2, H, T], F32R, 48 * KB)
        pc_l = at_("pc_l", [P, 2, H, T], F32R, 64 * KB)
        scores = ps("scores", [P, 2, 512])
        ptp = ps("ptp", [P, LT, 256])
        acc = ps("acc", [P, 2, 256])
        gb = [ps(f"gb{i}", [P, 2, 256]) for i in range(BANKS)]

        wa_in, wb_in, x_in, out_done, scratch_in = (
            sem(n) for n in ("wa_in", "wb_in", "x_in", "out_done", "scratch_in"))
        tailc_in = [sem(f"tailc_in{i}") for i in range(2)]
        ctxt_in = [sem(f"ctxt_in{i}") for i in range(2)]
        ctxn_in = [sem(f"ctxn_in{i}") for i in range(2)]
        bank_filled = [sem(f"bank_filled{i}") for i in range(BANKS)]
        bank_drained = [sem(f"bank_drained{i}") for i in range(BANKS)]
        names = ("wa_ready wb_hi wb_lo wz_ready wz_psum tail_split thi_ready tlo_ready nhi_ready nlo_ready "
                 "scores_ready nmax_ready exp_ready probs_ready tailp_ready tailt_ready ptt_ready pt_ready "
                 "pth_ready ptl_ready acc_ready pch_ready pcl_ready xthi_ready qhi_ready qkhi_ready "
                 "oh_ready xb_ready ob_ready var_ready rstd_ready xn_ready tanh_ready f_ready "
                 "inv_ready pw_ready hat_ready khat1_ready dve_chain pool_chain").split()
        s = {n: sem(n) for n in names}

        x_v = a["x"].rearrange("(g t p) d -> g p t d", g=NG, p=P)
        out_v = out.rearrange("(g t p) d -> g p t d", g=NG, p=P)
        ctxt_v, ctxn_v = a["ctx_t"], a["ctx_n"]
        scratch = nc.dram_tensor("tail_scratch", [3, B, 256], F32, kind="Internal").ap()

        wq_raw = at_("wq_raw", [P, 2, INNER], F32, 16 * KB)
        wo_raw = at_("wo_raw", [P, 4, D], F32, 0)
        wk_raw = at_("wk_raw", [P, H, 256], F32, 24 * KB)
        wv_raw = at_("wv_raw", [P, 2, H, P], F32, 4 * KB)
        wxt_raw = at_("wxt_raw", [P, 2, D], F32, 12 * KB)
        ww_raw = at_("ww_raw", [P, 2, D], F32, 14 * KB)
        tail_raw = at_("tail_raw", [P, C], F32, 44 * KB)
        tail3 = at_("tail3", [P, 3, 256], F32R, 48 * KB)
        bw_raw = at_("bw_raw", [P, 2], F32, 52 * KB)
        ident_raw = at_("ident_raw", [P, P], F32, 53 * KB)
        mask_raw = at_("mask_raw", [P, LEVELS, P], F32, 54 * KB)

        LOADS_A = [(tail_raw[:], a["ctx_tail"]), (wq_raw[:], a["wq"]), (ident_raw[:], a["ident"]),
                   (wk_raw[:], a["wk"]), (bw_raw[:], a["bw"]), (mask_raw[:], a["mask"])]
        LOADS_B = [(bo[:], a["bo"]), (wo_raw[:], a["wo"]), (wv_raw[:], a["wv"]), (wxt_raw[:], a["wxt"]),
                   (ww_raw[:], a["ww"]), (w2[:, 0], a["wk2"]), (w2[:, 1], a["wv2"]), (w2[:, 2], a["wr2"]),
                   (wo2[:], a["wo2"]), (u1[:], a["u1"]), (v1, a["v1"]), (u2[:], a["u2"]), (v2, a["v2"]),
                   (b2[:], a["b2"]), (vecs[:, 0:2], a["ln_g"]), (vecs[:, 2:4], a["ln_b"]),
                   (vecs[:, 6:14], a["b1"])]
        W_A, W_B = 16 * len(LOADS_A), 16 * len(LOADS_B)

        block = ctx.enter_context(nc.Block())

        def turns(engine, body):
            body(Phase("a", 0))
            body(Phase("ab", 0))
            with engine.Fori(0, NG - 2) as m:
                body(Phase("abc", m))
            body(Phase("bc", 0))
            body(Phase("c", 0))

        @block.sync
        def _(sp):
            for dst, src in LOADS_A:
                sp.dma_start(dst, src).then_inc(wa_in, 16)

            def body(ph):
                g = ph.a
                first = ph.which == "a"

                def load_t(b):
                    if not (first and b < 2):
                        sp.wait_ge(s["tlo_ready"], g.at(G, b - 1))
                    sp.dma_start(raw_t[b % 2][:], ctxt_v[g.index * G + b]).then_inc(ctxt_in[b % 2], 16)

                def load_n(b):
                    if not (first and b < 2):
                        sp.wait_ge(s["nlo_ready"], g.at(G, b - 1))
                    sp.dma_start(raw_n[b % 2][:], ctxn_v[g.index * G + b]).then_inc(ctxn_in[b % 2], 16)

                def load_tails(pair):
                    if not (first and pair < 2):
                        sp.wait_ge(s["acc_ready"], g.at(G, 2 * pair - 2))
                    i = 2 * (pair % 2)
                    sp.dma_start(tailc[:, i:i + 2].bitcast(F32), scratch[:, bass.ds(g.index * G + 2 * pair, 2)])\
                        .then_inc(tailc_in[pair % 2], 16)

                if not first:
                    sp.wait_ge(s["xb_ready"], g.at(1, 0))
                sp.dma_start(xin[:], x_v[g.index]).then_inc(x_in, 16)
                load_t(0)
                load_t(1)
                load_n(0)
                load_n(1)
                if first:
                    sp.wait_ge(scratch_in, 16)
                load_tails(0)
                load_tails(1)
                for b in range(2, G):
                    load_t(b)
                    load_n(b)
                    if b in (4, 6):
                        load_tails(b // 2)

            body(Phase("a", 0))
            body(Phase("ab", 0))
            with sp.Fori(0, NG - 2) as m:
                body(Phase("abc", m))

        @block.tensor
        def _(pe):
            mm = nc.tensor.matmul

            def body(ph):
                ga, gp, gc = ph.a, ph.b, ph.c
                taken = []

                def wz_product():
                    pe.wait_ge(wb_in, W_B)
                    for i in range(2):
                        for j in range(2):
                            last = mm(gb[3][:, i], wxt_raw[:, j, i * P:(i + 1) * P], ww_raw[:, j], start=j == 0,
                                      stop=j == 1)
                    last.then_inc(s["wz_psum"], 1)

                if ph.which == "a":
                    pe.wait_ge(s["wa_ready"], 1)
                if ph.which == "ab":
                    pe.wait_ge(s["wb_lo"], 1)
                    pe.wait_ge(s["wz_ready"], 1)

                def tile(name):
                    bank = bank_of(ph, name)
                    taken.append(name)
                    before = filled(ph, name, 0)
                    if not (isinstance(before, int) and before == 0):
                        pe.wait_ge(bank_drained[bank], before)
                    return gb[bank]

                def done(name, last):
                    last.then_inc(bank_filled[bank_of(ph, name)], 1)

                def drained(name):
                    order = order_of(ph.which)
                    ahead = order.index(taken[-1]) - order.index(name) if taken else 0
                    if ahead > 0 and ahead % BANKS == 0:
                        return
                    pe.wait_ge(bank_drained[bank_of(ph, name)], filled(ph, name))

                def turn(name):
                    ln = 0 if name == "XT" else int(name[2]) - 1
                    x_ = xn3 if ln == 2 else xn
                    out_ = tile(name)
                    pe.wait_ge(s["xn_ready"], norms_done(ph, ln))
                    for t in range(2):
                        for c in range(2):
                            last = nc.tensor.transpose(out_[:, c, t * P:(t + 1) * P],
                                                       x_[:, t, c * P:(c + 1) * P], ident)
                    done(name, last)

                def q(p):
                    out_ = tile(f"q{p}")
                    drained("XT")
                    k = 0
                    for c in range(2):
                        for w, x in ((wq_h, xth), (wq_l, xth), (wq_h, xtl)):
                            last = mm(out_[:, 0], w[:, c, p * P:(p + 1) * P], x[:, c], start=k == 0,
                                      stop=k == 5)
                            k += 1
                    done(f"q{p}", last)

                def qk(h):
                    out_ = tile(f"Qk{h}")
                    drained(f"q{h // 2}")
                    for c in range(2):
                        for k, w in enumerate((wk_h, wk_l)):
                            last = mm(out_[:, c], w[:, h, c * P:(c + 1) * P], qs[:, h % 4], start=k == 0,
                                      stop=k == 1)
                    done(f"Qk{h}", last)

                def score(b):
                    pe.wait_ge(s["tlo_ready"], ga.at(G, b + 1))
                    if b == 0:
                        drained("Qk7")
                    if not (ph.which == "a" and b == 0):
                        pe.wait_ge(s["exp_ready"], ga.at(2 * G, 2 * b))
                    if b > 1 or b == 1 and ph.which != "a":
                        pe.wait_ge(s["ptt_ready"], ga.at(G, b - 1))
                    for r in range(2):
                        o = scores[:, r, 0:LP]
                        r_ = slice(r * P, (r + 1) * P)
                        k = 0
                        for w, x in ((qk_h[:, 0, b, r_], t0h), (qk_l[:, 0, b, r_], t0h),
                                     (qk_h[:, 0, b, r_], t0l), (qk_h[:, 1, b, r_], t1),
                                     (qk_l[:, 1, b, r_], t1)):
                            last = mm(o, w, x[b % 2][:], start=k == 0, stop=k == 4)
                            k += 1
                        if b > 0:
                            last = turn_tail(b - 1, r)
                        last.then_inc(s["scores_ready"], 1)

                def turn_tail(b, r):
                    if r == 0:
                        pe.wait_ge(s["tailp_ready"], ga.at(G, b + 1))
                    return mm(scores[:, r, 384:512], tailp[:, r], ident_r[:], start=True, stop=True)

                def turn_probs(b):
                    pe.wait_ge(s["probs_ready"], ga.at(G, b + 1))
                    if not (ph.which == "a" and b == 0):
                        pe.wait_ge(s["ptl_ready"], ga.at(G, b))
                    for r in range(2):
                        for t in range(LT):
                            last = nc.tensor.transpose(ptp[:, t, r * P:(r + 1) * P],
                                                       probs[:, r, t * P:(t + 1) * P], ident)
                    last.then_inc(s["pt_ready"], 1)

                def pv(b):
                    pe.wait_ge(s["ptl_ready"], ga.at(G, b + 1))
                    pe.wait_ge(s["nlo_ready"], ga.at(G, b + 1))
                    if b % 2 == 0:
                        pe.wait_ge(tailc_in[b // 2 % 2], ga.at(16 * G // 4, 16 * (b // 4 + 1)))
                    if not (ph.which == "a" and b == 0):
                        pe.wait_ge(s["pcl_ready"], ga.at(G, b))
                    n = nat[b % 2]
                    terms = [(0, n[:, t, lo:lo + P], p_[:, t]) for t in range(LT)
                             for lo, p_ in ((0, pth), (0, ptl), (256, pth))]
                    terms += [(1, n[:, t, P:2 * P], p_[:, t]) for t in range(LT) for p_ in (pth, ptl)]
                    terms += [(i, tailc[:, b % 4, i * P:(i + 1) * P], ptt[:]) for i in range(2)]
                    for k, (i, w, x) in enumerate(terms):
                        if k == len(terms) - 2:
                            pe.wait_ge(s["ptt_ready"], ga.at(G, b + 1))
                        last = mm(acc[:, i], w, x, start=k == 0, stop=k == len(terms) - 1)
                    last.then_inc(s["acc_ready"], 1)

                def wv(p):
                    out_ = tile(f"WV{p}")
                    if p == 0:
                        pe.wait_ge(s["pcl_ready"], gp.at(G, G))
                    for i in range(2):
                        h0 = 4 * p + 2 * i
                        terms = [(w[:, c, h], x[:, c, h]) for h in (h0, h0 + 1) for c in range(2)
                                 for w, x in ((wv_h, pc_h), (wv_l, pc_h), (wv_h, pc_l))]
                        for k, (w, x) in enumerate(terms):
                            last = mm(out_[:, i], w, x, start=k == 0, stop=k == len(terms) - 1)
                    done(f"WV{p}", last)

                def y1():
                    out_ = tile("Y1")
                    drained("WV1")
                    for t in range(2):
                        t_ = slice(t * P, (t + 1) * P)
                        terms = [(o[:, p, t_], w[:, p]) for p in range(4)
                                 for o, w in ((oh, wo_h), (ol, wo_h), (oh, wo_l))]
                        for k, (w, x) in enumerate(terms):
                            last = mm(out_[:, t], w, x, start=k == 0, stop=k == len(terms) - 1)
                    done("Y1", last)

                def project(name):
                    w = {"z": wz, "k": w2[:, 0], "r": w2[:, 2]}[name]
                    out_ = tile(name)
                    drained("XT2")
                    for o in range(2):
                        for c in range(2):
                            last = mm(out_[:, o], w[:, c, o * P:(o + 1) * P], xt[:, c], start=c == 0,
                                      stop=c == 1)
                    done(name, last)

                def v():
                    out_ = tile("v")
                    for t in range(2):
                        for c in range(2):
                            last = mm(out_[:, t], xt[:, c, t * P:(t + 1) * P], w2[:, 1, c], start=c == 0,
                                      stop=c == 1)
                    done("v", last)

                def s_tile(name):
                    j, l0 = int(name[2]), 0 if name[1] == "a" else 2
                    t, rows = j // 2, slice(64 * (j % 2), 64 * (j % 2) + 64)
                    out_ = tile(name)
                    if j == 0:
                        pe.wait_ge(s["hat_ready"], hats_done(gp, "k0", "k3")[l0 // 2])
                        if l0 == 0:
                            pe.wait_ge(s["khat1_ready"], gp.at(1, 1))
                    for c in range(2):
                        cols = slice(c * T + t * P, c * T + t * P + P)
                        for l in range(2):
                            last = mm(out_[:, c, l * P:(l + 1) * P], khat[rows, l0 + l, cols],
                                      rhat[rows, l0 + l, cols], start=True, stop=True)
                    done(name, last)

                def o2_():
                    out_ = tile("O2")
                    drained("Sb3")
                    drained("v")
                    for j in range(8):
                        t, h = j // 4, j % 4
                        r0 = 64 * (h % 2)
                        last = mm(out_[r0:r0 + 64, h // 2, t * P:(t + 1) * P],
                                  vt[:, t, h * 64:(h + 1) * 64], s2[:, j], start=True, stop=True)
                    done("O2", last)

                def y2():
                    out_ = tile("Y2")
                    drained("O2")
                    for t in range(2):
                        for c in range(2):
                            last = mm(out_[:, t], o2[:, c, t * P:(t + 1) * P], wo2[:, c], start=c == 0,
                                      stop=c == 1)
                    done("Y2", last)

                def pf_():
                    out_ = tile("Pf")
                    drained("XT3")
                    for c in range(2):
                        last = mm(out_[0:R, 0], u1[:, c], xt3[:, c], start=c == 0, stop=c == 1)
                    done("Pf", last)

                def hidden(i):
                    out_ = tile(f"H{i}")
                    drained("Pf")
                    for c in range(2):
                        f = (2 * i + c) * P
                        last = mm(out_[:, c], v1[:, f:f + P], pf, start=True, stop=True)
                    done(f"H{i}", last)

                def qf_():
                    out_ = tile("Qf")
                    drained("H3")
                    for c in range(8):
                        last = mm(out_[0:R, 0], u2[:, c], hid[:, c], start=c == 0, stop=c == 7)
                    done("Qf", last)

                def y3():
                    out_ = tile("Y3")
                    drained("Qf")
                    for t in range(2):
                        last = mm(out_[:, t], qf[:, t * P:(t + 1) * P], v2, start=True, stop=True)
                    done("Y3", last)

                steps = {"Y1": y1, "v": v, "O2": o2_, "Y2": y2, "Pf": pf_, "Qf": qf_, "Y3": y3}
                for n in ("XT", "XT2", "XT3"):
                    steps[n] = lambda n=n: turn(n)
                for i in range(2):
                    steps[f"WV{i}"] = lambda i=i: wv(i)
                for n in "zkr":
                    steps[n] = lambda n=n: project(n)
                for i in range(8):
                    steps[f"Qk{i}"] = lambda i=i: qk(i)
                for i in range(4):
                    for n in (f"Sa{i}", f"Sb{i}"):
                        steps[n] = lambda n=n: s_tile(n)
                    steps[f"q{i}"] = lambda i=i: q(i)
                    steps[f"H{i}"] = lambda i=i: hidden(i)

                for n in START:
                    if ph.has(n):
                        steps[n]()
                if ga:
                    score(0)
                for n in AFTER_SCORE:
                    if ph.has(n):
                        steps[n]()
                for b in range(G):
                    if ga:
                        turn_probs(b)
                        if b + 1 < G:
                            score(b + 1)
                        else:
                            for r in range(2):
                                last = turn_tail(b, r)
                            last.then_inc(s["tailt_ready"], 1)
                    for n in FILL1[b]:
                        if ph.has(n):
                            steps[n]()
                    if ga:
                        pv(b)
                    for n in FILL2[b]:
                        if ph.has(n):
                            steps[n]()
                    if ph.which == "a" and b == 3:
                        wz_product()

            turns(pe, body)

        @block.scalar
        def _(act):
            go = nc.scalar.activation

            def body(ph):
                ga, gp, gc = ph.a, ph.b, ph.c

                def wait_tile(name):
                    bank = bank_of(ph, name)
                    act.wait_ge(bank_filled[bank], filled(ph, name))
                    return gb[bank]

                def drain(name, last):
                    last.then_inc(bank_drained[bank_of(ph, name)], 1)

                def t_hi(b):
                    act.wait_ge(ctxt_in[b % 2], ga.at(16 * G // 2, 16 * (b // 2 + 1)))
                    if not (ph.which == "a" and b < 2):
                        act.wait_ge(s["scores_ready"], ga.at(2 * G, 2 * (b - 1)))
                    go(t0h[b % 2][:], raw_t[b % 2][:, 0], ACT.Copy)
                    if not (ph.which == "a" and b < 1):
                        act.wait_ge(s["tlo_ready"], ga.at(G, b))
                    go(t1s[64:128], raw_t[b % 2][64:128, 1], ACT.Copy).then_inc(s["thi_ready"], 1)

                def n_hi(b):
                    act.wait_ge(ctxn_in[b % 2], ga.at(16 * G // 2, 16 * (b // 2 + 1)))
                    if not (ph.which == "a" and b < 2):
                        act.wait_ge(s["acc_ready"], ga.at(G, b - 1))
                    go(nat[b % 2][:, :, 0:C], raw_n[b % 2][:], ACT.Copy).then_inc(s["nhi_ready"], 1)

                def exps(b):
                    for r in range(2):
                        act.wait_ge(s["nmax_ready"], ga.at(2 * G, 2 * b + r + 1))
                        go(probs[:, r, 0:L], scores[:, r, 0:L], ACT.Exp, bias=nmax[:, r:r + 1],
                           accum_out=rsum[:, r:r + 1]).then_inc(s["exp_ready"], 1)
                    if b > 0:
                        tail_out(b - 1)

                def tail_out(b):
                    go(ptt[:].rearrange("a (r q) -> a r q", r=2), scores[0:3, :, 384:512], ACT.Copy)\
                        .then_inc(s["ptt_ready"], 1)

                def pt_hi(b):
                    act.wait_ge(s["pt_ready"], ga.at(G, b + 1))
                    go(pth[:], ptp[:], ACT.Copy).then_inc(s["pth_ready"], 1)

                def pc_hi(b):
                    act.wait_ge(s["acc_ready"], ga.at(G, b + 1))
                    go(pc_h[:, :, :, b * S:(b + 1) * S], acc[:].rearrange("p c (h s) -> p c h s", h=H),
                       ACT.Copy).then_inc(s["pch_ready"], 1)

                def step(n):
                    if n in ("Y1", "Y2", "Y3") or n[0] == "S":
                        return
                    t = wait_tile(n)
                    if n == "XT":
                        go(xth[:], t[:], ACT.Copy).then_inc(s["xthi_ready"], 1)
                    elif n == "XT2":
                        for c in range(2):
                            last = go(xt[:, c], t[:, c], ACT.Identity, scale=vecs[:, c:c + 1],
                                      bias=vecs[:, 2 + c:3 + c])
                        drain(n, last)
                    elif n == "XT3":
                        drain(n, go(xt3[:], t[:], ACT.Copy))
                    elif n[0] == "q":
                        p = int(n[1])
                        for i in range(2):
                            last = go(qs[0:64, (2 * p + i) % 4], t[64 * i:64 * i + 64, 0], ACT.Copy)
                        last.then_inc(s["qhi_ready"], 1)
                    elif n[:2] == "Qk":
                        h = int(n[2])
                        go(qk_h[:, :, :, h * S:(h + 1) * S],
                           t[:].rearrange("p c (b s) -> p c b s", b=G), ACT.Copy)\
                            .then_inc(s["qkhi_ready"], 1)
                    elif n[:2] == "WV":
                        go(oh[:, 2 * int(n[2]):2 * int(n[2]) + 2], t[:], ACT.Copy).then_inc(s["oh_ready"], 1)
                    elif n == "z":
                        for c in range(2):
                            last = go(at[:, c], t[:, c], ACT.Tanh, scale=0.5, bias=vecs[:, 4 + c:5 + c])
                        last.then_inc(s["tanh_ready"], 1)
                        act.wait_ge(s["tanh_ready"], gp.at(2, 1))
                        drain(n, go(at[:], at[:], ACT.Copy, scale=-0.5, bias=0.5))
                    elif n == "r":
                        go(rt_[:], t[:], ACT.Tanh, scale=0.5).then_inc(s["tanh_ready"], 1)
                        act.wait_ge(s["tanh_ready"], gp.at(2, 2))
                        drain(n, go(rt_[:], rt_[:], ACT.Copy, scale=0.5, bias=0.5))
                    elif n == "k":
                        drain(n, go(kt[:], t[:], ACT.Copy))
                    elif n == "v":
                        if gc:
                            act.wait_ge(out_done, gc.at(16, 16))
                        drain(n, go(vt[:], t[:], ACT.Copy))
                    elif n == "O2":
                        drain(n, go(o2, t[:], ACT.Copy))
                    elif n == "Pf":
                        drain(n, go(pf, t[0:R, 0], ACT.Copy))
                    elif n[0] == "H":
                        i = int(n[1])
                        for c in range(2):
                            f = 2 * i + c
                            last = go(hid[:, f], t[:, c], ACT.Gelu_apprx_tanh, bias=vecs[:, 6 + f:7 + f])
                        drain(n, last)
                    elif n == "Qf":
                        drain(n, go(qf, t[0:R, 0], ACT.Copy))

                if ga:
                    t_hi(0)
                for n in START:
                    if ph.has(n):
                        step(n)
                    if n == "XT3" and ga:
                        t_hi(1)
                        n_hi(0)
                if ga:
                    exps(0)
                for n in AFTER_SCORE:
                    if ph.has(n):
                        step(n)
                for b in range(G):
                    if ga:
                        pt_hi(b)
                        if b + 2 < G:
                            t_hi(b + 2)
                        if b + 1 < G:
                            n_hi(b + 1)
                            exps(b + 1)
                        else:
                            act.wait_ge(s["tailt_ready"], ga.at(1, 1))
                            tail_out(b)
                    for n in FILL1[b]:
                        if ph.has(n):
                            step(n)
                    if ga:
                        pc_hi(b)
                    for n in FILL2[b]:
                        if ph.has(n):
                            step(n)
                    if ph.which == "a" and b == 1:
                        act.wait_ge(wb_in, W_B)
                        go(wo_h[:], wo_raw[:], ACT.Copy)
                        go(wv_h[:], wv_raw[:], ACT.Copy).then_inc(s["wb_hi"], 1)
                    if gc and b == 1:
                        act.wait_ge(bank_drained[bank_of(ph, "Y3")], filled(ph, "Y3"))
                        act.dma_start(out_v[gc.index], ob[:]).then_inc(out_done, 16)

            act.wait_ge(wa_in, W_A)
            for dst, src in LOADS_B:
                act.dma_start(dst, src).then_inc(wb_in, 16)
            act.wait_ge(s["tail_split"], 1)
            act.dma_start(scratch.rearrange("r b c -> b r c"), tail3[:].bitcast(F32)).then_inc(scratch_in, 16)
            act.wait_ge(s["wa_ready"], 1)
            turns(act, body)
            act.wait_ge(out_done, 16 * NG)

        @block.vector
        def _(dve):
            v_ = nc.vector
            chain = Chain(dve, s["dve_chain"], DVE_SETUP, DVE_LINKS)
            link, sign, need = chain.link, chain.sign, chain.need

            for buf in (tailp[:].bitcast(F32), s2[:], tail3[:].bitcast(F32)):
                v_.memset(buf, 0.0)
            v_.memset(vecs[:, 14:16], -0.5)
            v_.memset(eps2[:], EPS)
            v_.memset(probs[:], 0.0)
            v_.memset(t1s[0:64].bitcast(F32), 0.0)
            link(v_.memset(fw[:], 1.0))
            dve.wait_ge(wa_in, W_A)
            link(v_.tensor_copy(tail3[:, 0, 0:C], tail_raw[:]))
            v_.tensor_copy(tail3[:, 2, 0:C], tail_raw[:])
            v_.tensor_tensor(tail3[:, 1, 0:P], tail_raw[:, 0:P], tail3[:, 0, 0:P].bitcast(F32), ALU.subtract)
            for i in (0, 2):
                last = v_.tensor_tensor(tail3[:, i, C:256], tail_raw[:, P:C], tail3[:, 0, P:C].bitcast(F32),
                                        ALU.subtract)
            last.then_inc(s["tail_split"], 1)
            v_.tensor_copy(ident_r[:], ident_raw[:])
            v_.tensor_copy(mask[:], mask_raw[:])
            v_.tensor_scalar(vecs[:, 4:6], bw_raw[:], 0.5, None, ALU.mult)
            v_.tensor_copy(wq_h[:], wq_raw[:])
            link(v_.tensor_scalar(wk_h[:], wk_raw[:], SCALE, None, ALU.mult))
            v_.tensor_tensor(wq_l[:], wq_raw[:], wq_h[:].bitcast(F32), ALU.subtract)
            v_.scalar_tensor_tensor(wk_l[:], wk_raw[:], SCALE, wk_h[:].bitcast(F32), ALU.mult, ALU.subtract)\
                .then_inc(s["wa_ready"], 1)
            assert chain.k == DVE_SETUP, chain.k

            def body(ph):
                ga, gp, gc = ph.a, ph.b, ph.c
                chain.begin(ph)
                held, marks = [], {}

                def wait_tile(name):
                    bank = bank_of(ph, name)
                    dve.wait_ge(bank_filled[bank], filled(ph, name))
                    return gb[bank]

                def drain(name, last):
                    last.then_inc(bank_drained[bank_of(ph, name)], 1)

                def own_drain(name):
                    dve.wait_ge(bank_drained[bank_of(ph, name)], filled(ph, name))

                def hold(k=0):
                    if held or k:
                        need(max([k] + held))
                    held.append(sign(v_.memset(cell[:], 0.0)))

                def norm_stats(x, ln):
                    v_.bn_stats(stats[:, 0], x[:, 0])
                    hold(sign(v_.bn_stats(stats[:, 1], x[:, 1])))
                    for t in range(2):
                        last = v_.bn_aggr(mv[:, ln, t], stats[:, t])
                    link(last)
                    v_.tensor_scalar(ve[:, ln], mv[:, ln, :, 1], EPS, None, ALU.add)\
                        .then_inc(s["var_ready"], 1)

                def norm_apply(x, ln):
                    dve.wait_ge(s["rstd_ready"], norms_done(ph, ln))
                    k = 3 if ln == 1 else ln
                    xn_ = xn3 if ln == 2 else xn
                    for t in range(2):
                        last = v_.tensor_scalar(xn_[:, t], x[:, t], mv[:, ln, t, 0:1], rstd[:, k, t:t + 1],
                                                ALU.subtract, ALU.mult)
                    last.then_inc(s["xn_ready"], 1)

                def nmaxs(b):
                    for r in range(2):
                        dve.wait_ge(s["scores_ready"], ga.at(2 * G, 2 * b + r + 1))
                        v_.tensor_reduce(nmax[:, r:r + 1], scores[:, r, 0:L], AX.X, ALU.max, negate=True)\
                            .then_inc(s["nmax_ready"], 1)

                def norm_probs(b):
                    dve.wait_ge(s["exp_ready"], ga.at(2 * G, 2 * b + 2))
                    link(v_.reciprocal(rinv[:], rsum[:]))
                    for r in range(2):
                        last = v_.tensor_scalar(probs[:, r, 0:L], probs[:, r, 0:L], rinv[:, r:r + 1], None,
                                                ALU.mult)
                    last.then_inc(s["probs_ready"], 1)

                def tail_parts(b):
                    dve.wait_ge(s["probs_ready"], ga.at(G, b + 1))
                    link(v_.tensor_copy(tailp[:, :, 0:2], probs[:, :, L - 1:L].to_broadcast([P, 2, 2])))
                    v_.tensor_tensor(tailp[:, :, 2:3], probs[:, :, L - 1:L], tailp[:, :, 0:1].bitcast(F32),
                                     ALU.subtract).then_inc(s["tailp_ready"], 1)

                def pt_lo(b):
                    dve.wait_ge(s["pth_ready"], ga.at(G, b + 1))
                    v_.tensor_tensor(ptl[:], ptp[:], pth[:].bitcast(F32), ALU.subtract)\
                        .then_inc(s["ptl_ready"], 1)

                def pc_lo(b):
                    dve.wait_ge(s["pch_ready"], ga.at(G, b + 1))
                    b_ = slice(b * S, (b + 1) * S)
                    v_.tensor_tensor(pc_l[:, :, :, b_], acc[:].rearrange("p c (h s) -> p c h s", h=H),
                                     pc_h[:, :, :, b_].bitcast(F32), ALU.subtract)\
                        .then_inc(s["pcl_ready"], 1)

                def decay_step(n):
                    a_flat = at[:].rearrange("p c t -> p (c t)")
                    k_flat = kt[:].rearrange("p c t -> p (c t)")
                    a4, f4, b4, p4 = (x.rearrange("p (n i) -> p n i", i=4)
                                      for x in (a_flat, fw[:], bw_[:], pw[:]))

                    def two(x, l):
                        return x.rearrange("p (m h i) -> p m h i", h=2, i=2 << l)

                    i = int(n[1]) if n[-1].isdigit() else 0
                    if n == "f1":
                        dve.wait_ge(bank_drained[bank_of(ph, "z")], filled(ph, "z"))
                        marks[n] = sign(v_.tensor_scalar(f4[:, :, 1:2], a4[:, :, 1:2], A_MIN, None, ALU.max))
                    elif n[0] == "f":
                        need(marks[f"f{i - 1}"])
                        out_ = v_.scalar_tensor_tensor(f4[:, :, i:i + 1], a4[:, :, i:i + 1], A_MIN,
                                                       f4[:, :, i - 1:i], ALU.max, ALU.mult)
                        if i == 3:
                            out_.then_inc(s["f_ready"], 1)
                        else:
                            marks[n] = sign(out_)
                    elif n[0] == "i":
                        if i == 1:
                            v_.memset(b4[:, :, 0:1], 1.0)
                        if i == 3:
                            dve.wait_ge(s["f_ready"], gp.at(1, 1))
                        else:
                            need(marks[f"f{i}"])
                        out_ = v_.reciprocal(b4[:, :, i:i + 1], f4[:, :, i:i + 1])
                        if i == 3:
                            out_.then_inc(s["inv_ready"], 1)
                    elif n == "pw":
                        dve.wait_ge(s["f_ready"], gp.at(1, 1))
                        v_.scalar_tensor_tensor(p4, a4[:, :, 0:1].to_broadcast([P, T // 2, 4]), A_MIN, f4,
                                                ALU.max, ALU.mult).then_inc(s["pw_ready"], 1)
                    elif n == "bw":
                        dve.wait_ge(s["inv_ready"], gp.at(1, 1))
                        dve.wait_ge(s["pw_ready"], gp.at(LEVELS - 1, 1))
                        marks[n] = sign(v_.tensor_tensor(a4, b4, f4[:, :, 3:4].to_broadcast([P, T // 2, 4]),
                                                         ALU.mult))
                    elif n == "k1":
                        dve.wait_ge(bank_drained[bank_of(ph, "k")], filled(ph, "k"))
                        need(marks["bw"])
                        v_.tensor_tensor(khat[:, 1], k_flat, a_flat, ALU.mult).then_inc(s["khat1_ready"], 1)
                    elif n[0] == "b":
                        if i == 1:
                            dve.wait_ge(s["khat1_ready"], gp.at(1, 1))
                        else:
                            dve.wait_ge(s["hat_ready"], hats_done(gp, "k2")[0])
                        b_, p_ = two(a_flat, i), two(pw[:], i)
                        marks[n] = sign(v_.tensor_tensor(
                            b_[:, :, 0], b_[:, :, 0],
                            p_[:, :, 1, (2 << i) - 1:2 << i].to_broadcast([P, 2 * T // (4 << i), 2 << i]),
                            ALU.mult))
                    else:
                        dve.wait_ge(s["hat_ready"], hats_done(gp, f"r{i}")[0])
                        need(marks[f"b{i}"])
                        p_ = two(pw[:], i)
                        v_.tensor_tensor(p_[:, :, 1], p_[:, :, 1],
                                         p_[:, :, 0, (2 << i) - 1:2 << i].to_broadcast(
                                             [P, 2 * T // (4 << i), 2 << i]),
                                         ALU.mult).then_inc(s["pw_ready"], 1)

                def step(n):
                    if n == "XT":
                        t = wait_tile(n)
                        dve.wait_ge(s["xthi_ready"], ga.at(1, 1))
                        drain(n, v_.tensor_tensor(xtl[:], t[:], xth[:].bitcast(F32), ALU.subtract))
                    elif n[0] == "q":
                        p = int(n[1])
                        t = wait_tile(n)
                        dve.wait_ge(s["qhi_ready"], ga.at(4, p + 1))
                        for i in range(2):
                            h = (2 * p + i) % 4
                            last = v_.tensor_tensor(qs[64:128, h], t[64 * i:64 * i + 64, 0],
                                                    qs[0:64, h].bitcast(F32), ALU.subtract)
                        drain(n, last)
                    elif n[:2] == "Qk":
                        h = int(n[2])
                        t = wait_tile(n)
                        dve.wait_ge(s["qkhi_ready"], ga.at(H, h + 1))
                        h_ = slice(h * S, (h + 1) * S)
                        drain(n, v_.tensor_tensor(qk_l[:, :, :, h_], t[:].rearrange("p c (b s) -> p c b s", b=G),
                                                  qk_h[:, :, :, h_].bitcast(F32), ALU.subtract))
                    elif n[:2] == "WV":
                        p = int(n[2])
                        t = wait_tile(n)
                        dve.wait_ge(s["oh_ready"], gp.at(2, p + 1))
                        p_ = slice(2 * p, 2 * p + 2)
                        drain(n, v_.tensor_tensor(ol[:, p_], t[:], oh[:, p_].bitcast(F32), ALU.subtract))
                    elif n == "Y1":
                        dve.wait_ge(s["xb_ready"], gp.at(1, 1))
                        if gc:
                            dve.wait_ge(s["ob_ready"], gc.at(1, 1))
                        drain(n, v_.tensor_tensor(x12[:], wait_tile(n)[:], xb[:], ALU.add))
                    elif n[0] == "S":
                        j, l0 = int(n[2]), 0 if n[1] == "a" else 2
                        t = wait_tile(n)
                        if l0:
                            own_drain(f"Sa{j}")
                        first = 4 * (j // 2) + j % 2
                        k = 0
                        for l in range(2):
                            hold(k)
                            i = v_.copy_predicated(
                                s2[:, first:first + 3:2],
                                mask[:, l0 + l:l0 + l + 1].to_broadcast([P, 2, P]), t[:, :, l * P:(l + 1) * P])
                            if l == 0:
                                k = sign(i)
                        drain(n, i)
                    elif n == "Y2":
                        bank, count = y2_before(ph)
                        dve.wait_ge(bank_filled[bank], count)
                        v_.tensor_tensor(x12[:], gb[bank][:], x12[:], ALU.add).then_inc(bank_drained[bank], 1)
                        dve.wait_ge(bank_drained[bank], count)
                        norm_stats(x12, 2)
                    elif n == "Y3":
                        t = wait_tile(n)
                        dve.wait_ge(s["ob_ready"], gc.at(1, 1))
                        drain(n, v_.tensor_tensor(ob[:], t[:], ob[:], ALU.add))
                    elif n in GAP_STEPS:
                        decay_step(n)

                def gap(b, i):
                    for n in GAPS[b][i]:
                        if gc if n == "Y3" else gp:
                            step(n)

                if ga:
                    dve.wait_ge(x_in, ga.at(16, 16))
                    norm_stats(xin, 0)
                if gc:
                    step("Y2")
                for n in START:
                    if n == "WV0" and ga:
                        norm_apply(xin, 0)
                    if n == "WV1" and gc:
                        norm_apply(x12, 2)
                    if n == "Qk1" and gp:
                        own_drain("Y1")
                        norm_stats(x12, 1)
                    if n == "q3" and gp:
                        norm_apply(x12, 1)
                    if ph.has(n):
                        step(n)
                if ga:
                    nmaxs(0)
                    norm_probs(0)
                    tail_parts(0)
                for b in range(G):
                    gap(b, 0)
                    if ga:
                        pt_lo(b)
                        if b + 1 < G:
                            nmaxs(b + 1)
                    gap(b, 1)
                    if ga and b + 1 < G:
                        norm_probs(b + 1)
                        tail_parts(b + 1)
                    gap(b, 2)
                    if ga:
                        pc_lo(b)
                    gap(b, 3)
                    if ph.which == "a" and b == 4:
                        dve.wait_ge(s["wz_psum"], 1)
                        v_.tensor_copy(wz[:], gb[3][:]).then_inc(s["wz_ready"], 1)
                if ph.which != "c":
                    assert chain.k == DVE_LINKS[ph.which], chain.k

            turns(dve, body)

        @block.gpsimd
        def _(pool):
            p_ = nc.gpsimd
            chain = Chain(pool, s["pool_chain"], 0, POOL_LINKS)

            def body(ph):
                ga, gp, gc = ph.a, ph.b, ph.c
                chain.begin(ph)
                link = chain.link
                half = vecs[:, 14:16]

                def t_lo(b):
                    pool.wait_ge(s["thi_ready"], ga.at(G, b + 1))
                    i = b % 2
                    p_.tensor_tensor(t0l[i][:], raw_t[i][:, 0], t0h[i][:].bitcast(F32), ALU.subtract)
                    p_.tensor_tensor(t1[i][:], raw_t[i][:, 1], t1s[:].bitcast(F32), ALU.subtract)\
                        .then_inc(s["tlo_ready"], 1)

                def n_lo(b):
                    pool.wait_ge(s["nhi_ready"], ga.at(G, b + 1))
                    i = b % 2
                    p_.tensor_tensor(nat[i][:, :, 256:384], raw_n[i][:, :, 0:P],
                                     nat[i][:, :, 0:P].bitcast(F32), ALU.subtract)
                    p_.tensor_tensor(nat[i][:, :, C:256], raw_n[i][:, :, P:C],
                                     nat[i][:, :, P:C].bitcast(F32), ALU.subtract)\
                        .then_inc(s["nlo_ready"], 1)

                def rstds(ln):
                    pool.wait_ge(s["var_ready"], norms_done(ph, ln))
                    i = p_.tensor_tensor(rstd[:, ln], ve[:, ln], half, ALU.pow)
                    if ln == 1:
                        link(i)
                        link(p_.tensor_tensor(rstd[:, 3], mv[:, 1, :, 1], rstd[:, 1], ALU.mult))
                        link(p_.tensor_tensor(rstd[:, 3], rstd[:, 3], rstd[:, 1], ALU.mult))
                        link(p_.tensor_tensor(rstd[:, 3], rstd[:, 3], eps2[:], ALU.add))
                        link(p_.tensor_tensor(rstd[:, 3], rstd[:, 3], half, ALU.pow))
                        i = p_.tensor_tensor(rstd[:, 3], rstd[:, 3], rstd[:, 1], ALU.mult)
                    i.then_inc(s["rstd_ready"], 1)

                def hat(n):
                    l = int(n[1])
                    if n[0] == "r":
                        if l == 0:
                            pool.wait_ge(bank_drained[bank_of(ph, "r")], filled(ph, "r"))
                            pool.wait_ge(s["f_ready"], gp.at(1, 1))
                        else:
                            pool.wait_ge(s["pw_ready"], gp.at(LEVELS - 1, l))
                        i = p_.tensor_tensor(rhat[:, l], rt_[:].rearrange("p c t -> p (c t)"),
                                             (pw if l else fw)[:], ALU.mult)
                    else:
                        if l == 0:
                            pool.wait_ge(bank_drained[bank_of(ph, "k")], filled(ph, "k"))
                            pool.wait_ge(s["inv_ready"], gp.at(1, 1))
                        if l == 3:
                            pool.wait_ge(bank_filled[bank_of(ph, "v")], filled(ph, "v"))
                        i = p_.tensor_tensor(khat[:, l], kt[:].rearrange("p c t -> p (c t)"),
                                             at[:].rearrange("p c t -> p (c t)") if l else bw_[:], ALU.mult)
                    i.then_inc(s["hat_ready"], 1)

                if ga:
                    rstds(0)
                if gc:
                    rstds(2)
                    p_.tensor_tensor(ob[:], x12[:], b2[:].rearrange("p (o d) -> p o d", o=1).to_broadcast([P, 2, D]),
                                     ALU.add).then_inc(s["ob_ready"], 1)
                if ga:
                    t_lo(0)
                if gp:
                    rstds(1)
                if ga:
                    t_lo(1)
                    n_lo(0)
                    pool.wait_ge(s["xn_ready"], norms_done(ph, 0))
                    if ph.which == "a":
                        pool.wait_ge(wb_in, W_B)
                    p_.tensor_tensor(xb[:], xin[:], bo[:].rearrange("p (o d) -> p o d", o=1).to_broadcast([P, 2, D]),
                                     ALU.add).then_inc(s["xb_ready"], 1)
                for b in range(G):
                    if gp:
                        for n in POOL_HATS[b][0]:
                            hat(n)
                    if ga:
                        if b + 2 < G:
                            t_lo(b + 2)
                        if b + 1 < G:
                            n_lo(b + 1)
                    if gp:
                        for n in POOL_HATS[b][1]:
                            hat(n)
                    if ph.which == "a":
                        if b == 2:
                            pool.wait_ge(s["wb_hi"], 1)
                            p_.tensor_tensor(wo_l[:], wo_raw[:], wo_h[:].bitcast(F32), ALU.subtract)
                        if b in (3, 4):
                            c = b - 3
                            i = p_.tensor_tensor(wv_l[:, c], wv_raw[:, c], wv_h[:, c].bitcast(F32), ALU.subtract)
                            if b == 4:
                                i.then_inc(s["wb_lo"], 1)
                if ph.which != "c":
                    assert chain.k == POOL_LINKS[ph.which], chain.k

            pool.wait_ge(s["wa_ready"], 1)
            turns(pool, body)


def hats_done(group, *names):
    return [group.at(HATS, HAT_ORDER.index(n) + 1) for n in names]


def norms_done(phase, ln):
    here = [l for l, group in ((0, phase.a), (2, phase.c), (1, phase.b)) if group]
    return phase.before({"a": 1, "ab": 2, "abc": 3, "bc": 2}.get) + here.index(ln) + 1


def level_masks():
    t = np.arange(P)
    key, query = t[:, None], t[None, :]
    masks = [(key // 4 == query // 4) & (key <= query)]
    for n in (4, 8, 16):
        masks.append((key // (2 * n) == query // (2 * n)) & (key // n < query // n))
    return np.stack(masks, 1).astype(np.float32)


def chunks(w, p=P):
    return np.ascontiguousarray(w.reshape(-1, p, w.shape[-1]).transpose(1, 0, 2))


def kernel(x, ctx_768, L0_xattn_Wq, L0_xattn_Wk, L0_xattn_Wv, L0_xattn_Wo, L0_xattn_bo, L0_attn_ln_g,
           L0_attn_ln_b, L0_attn_Wx, L0_attn_Ww, L0_attn_bw, L0_attn_Wk, L0_attn_Wv, L0_attn_Wr,
           L0_attn_Wo, L0_ffn_U1, L0_ffn_V1, L0_ffn_b1, L0_ffn_U2, L0_ffn_V2, L0_ffn_b2):
    import concourse.bacc as bacc
    from concourse.bass_utils import run_bass_kernel_spmd

    c = np.asarray(ctx_768)
    ctx_t = np.zeros((B, P, 2, LP), c.dtype)
    ct = c.transpose(0, 2, 1)
    ctx_t[:, :, 0, :L] = ct[:, :P]
    ctx_t[:, :64, 1, :L] = ct[:, P:]
    ctx_t[:, 64:, 1, :L] = ct[:, P:]
    ctx_n = np.ascontiguousarray(c[:, :LT * P].reshape(B, LT, P, C).transpose(0, 2, 1, 3))
    wk = np.asarray(L0_xattn_Wk).T.reshape(H, DH, C).transpose(1, 0, 2)
    wk = np.concatenate([wk, wk[:, :, P:]], 2)
    wk = np.concatenate([wk, wk], 0)
    wv_ = np.asarray(L0_xattn_Wv)
    wv = np.zeros((P, 2, H, P), wv_.dtype)
    for h in range(H):
        o = 64 * (h % 2)
        wv[:, 0, h, o:o + 64] = wv_[:P, h * 64:(h + 1) * 64]
        wv[:64, 1, h, o:o + 64] = wv_[P:, h * 64:(h + 1) * 64]
        wv[64:, 1, h, o:o + 64] = wv_[P:, h * 64:(h + 1) * 64]

    def column(v):
        return np.ascontiguousarray(np.asarray(v).reshape(-1, P).T)

    def rows(v):
        return np.ascontiguousarray(np.broadcast_to(np.asarray(v), (P, D)))

    arrays = {
        "x": np.ascontiguousarray(np.asarray(x).reshape(B * S, D)), "ctx_t": ctx_t, "ctx_n": ctx_n,
        "ctx_tail": np.ascontiguousarray(c[:, L - 1]),
        "wq": chunks(np.asarray(L0_xattn_Wq)), "wk": wk, "wv": wv, "wo": chunks(np.asarray(L0_xattn_Wo)),
        "bo": rows(L0_xattn_bo), "ln_g": column(L0_attn_ln_g), "ln_b": column(L0_attn_ln_b),
        "wxt": chunks(np.asarray(L0_attn_Wx).T), "ww": chunks(np.asarray(L0_attn_Ww)),
        "bw": column(L0_attn_bw), "wk2": chunks(np.asarray(L0_attn_Wk)),
        "wv2": chunks(np.asarray(L0_attn_Wv)), "wr2": chunks(np.asarray(L0_attn_Wr)),
        "wo2": chunks(np.asarray(L0_attn_Wo)), "u1": chunks(np.asarray(L0_ffn_U1)),
        "v1": np.asarray(L0_ffn_V1), "b1": column(L0_ffn_b1), "u2": chunks(np.asarray(L0_ffn_U2)),
        "v2": np.asarray(L0_ffn_V2), "b2": rows(L0_ffn_b2),
        "ident": np.eye(P, dtype=np.float32), "mask": level_masks(),
    }
    nc = bacc.Bacc("TRN2", target_bir_lowering=False, num_devices=1)
    a = {n: nc.dram_tensor(f"in_{n}", v.shape, mybir.dt.from_np(v.dtype), kind="ExternalInput").ap()
         for n, v in arrays.items()}
    out = nc.dram_tensor("out", (B * S, D), F32, kind="ExternalOutput").ap()
    build(nc, a, out)
    r = run_bass_kernel_spmd(nc, [{f"in_{n}": v for n, v in arrays.items()}], core_ids=[0])
    return r.results[0]["out"].reshape(B, S, D)
```
